# Optimizing a Trainium2 kernel written in Bass

```python
import numpy as np
import jax
import jax.numpy as jnp

def _softmax(x, axis=-1):
    return jax.nn.softmax(x, axis=axis)

def _gelu(x):
    return jax.nn.gelu(x, approximate=True)

def _silu(x):
    return jax.nn.silu(x)

def _sigmoid(x):
    return jax.nn.sigmoid(x)

def _layernorm(x, axis=-1, eps=1e-05):
    m = jnp.mean(x, axis=axis, keepdims=True)
    v = jnp.var(x, axis=axis, keepdims=True)
    return (x - m) / jnp.sqrt(v + eps)

def _scatter_add(tgt, idx, src, axis=0):
    return tgt.at[idx].add(src)

def _segment_sum(src, seg, n):
    return jax.ops.segment_sum(src, seg, n)
kernel_name = 'mk_xattn_ffn_d1_seqx_r4_f78b94'

def setup_inputs(seed: int=0):
    np.random.seed(seed)
    _w = jnp.asarray

    def _rec_inputs():
        import jax
        import jax.numpy as jnp
        _rk = jax.random.key(seed)
        x = 7.22e-05 + 1 * jax.random.normal(jax.random.fold_in(_rk, 1), (4, 512, 256), jnp.float32)
        _lenS = 512 - jax.random.randint(jax.random.fold_in(_rk, 7), (4,), 0, max(1, 512 // 4) + 1, jnp.int32)
        _lenS2 = 1024 - jax.random.randint(jax.random.fold_in(_rk, 8), (4,), 0, max(1, 1024 // 4) + 1, jnp.int32)
        _ctx_1024P = jax.random.normal(jax.random.fold_in(_rk, 11), (4, 16, 256), jnp.float32)
        _ctx_1024c = jax.random.dirichlet(jax.random.fold_in(_rk, 511), 0.3 * jnp.ones((16,), jnp.float32), (4, 1024))
        _ctx_1024t = jnp.einsum('bsk,bkd->bsd', _ctx_1024c, _ctx_1024P)
        _ctx_1024t = _ctx_1024t * jax.lax.rsqrt(jnp.mean(jnp.square(_ctx_1024t)) + 1e-12) * 0.953939
        ctx_1024 = 4.13588e-05 + 0.999923 * (_ctx_1024t + 0.3 * jax.random.normal(jax.random.fold_in(_rk, 611), (4, 1024, 256), jnp.float32))
        _validS = jnp.arange(512)[None, :] < _lenS[:, None]
        _validS2 = jnp.arange(1024)[None, :] < _lenS2[:, None]
        _causal = jnp.tril(jnp.ones((512, 512), dtype=bool))
        mask_BxS2_ik0 = jnp.where(jnp.broadcast_to(_validS2[:, :], (4, 1024)), 0, 1).astype(jnp.int32)
        return (x, ctx_1024, mask_BxS2_ik0)
    x, ctx_1024, mask_BxS2_ik0 = _rec_inputs()

    def _L0_xattn_setup():
        import jax, jax.numpy as jnp
        import numpy as np
        B, S, D, H = (4, 512, 256, 16)
        DK = D // H

        def _rope(x):
            s, d = (x.shape[-2], x.shape[-1])
            inv_freq = 1.0 / 10000.0 ** (jnp.arange(0, d, 2, dtype=jnp.float32) / d)
            angles = jnp.arange(s, dtype=jnp.float32)[:, None] * inv_freq[None, :]
            ang = jnp.repeat(angles, 2, axis=-1)
            cos, sin = (jnp.cos(ang), jnp.sin(ang))
            xp = x.reshape(*x.shape[:-1], d // 2, 2)
            rot = jnp.stack((-xp[..., 1], xp[..., 0]), axis=-1).reshape(x.shape)
            return x * cos + rot * sin
        key = jax.random.key(seed)
        ks = jax.random.split(key, 8)
        scale = 1.0 / np.sqrt(D)
        return {'q': jax.random.normal(ks[0], (B, S, D), dtype=jnp.float32), 'k': jax.random.normal(ks[1], (B, S, D), dtype=jnp.float32), 'v': jax.random.normal(ks[2], (B, S, D), dtype=jnp.float32), 'mask': jax.random.randint(ks[3], (B, S), 0, 2, dtype=jnp.int32), 'w_q': jax.random.normal(ks[4], (D, D), dtype=jnp.float32) * scale, 'w_k': jax.random.normal(ks[5], (D, D), dtype=jnp.float32) * scale, 'w_v': jax.random.normal(ks[6], (D, D), dtype=jnp.float32) * scale, 'w_o': jax.random.normal(ks[7], (D, D), dtype=jnp.float32) * scale}
    _L0_xattn_all = _L0_xattn_setup()
    _L0_xattn_in = {k: v for k, v in _L0_xattn_all.items() if k in ('w_q', 'w_k', 'w_v', 'w_o')}
    del _L0_xattn_all

    def _L0_ffn_setup():
        import jax, jax.numpy as jnp
        import numpy as np
        EPS = 1e-05
        NUM_HEADS = 16
        NUM_KV_HEADS = 4
        NUM_EXPERTS = 8
        TOP_K = 2

        def _layernorm(x, w, b):
            mu = jnp.mean(x, axis=-1, keepdims=True)
            var = jnp.mean((x - mu) ** 2, axis=-1, keepdims=True)
            return (x - mu) * jax.lax.rsqrt(var + EPS) * w + b
        key = jax.random.key(seed)
        ks = jax.random.split(key, 8)
        S, B, H = (256, 4, 256)
        F = 512
        hd = H // NUM_HEADS
        qkv_out = (NUM_HEADS + 2 * NUM_KV_HEADS) * hd
        w_scale = 0.02
        return {'hidden_states': jax.random.normal(ks[0], (S, B, H), jnp.float32), 'ln1_weight': jnp.ones((H,), jnp.float32), 'ln1_bias': jnp.zeros((H,), jnp.float32), 'ln2_weight': jnp.ones((H,), jnp.float32), 'ln2_bias': jnp.zeros((H,), jnp.float32), 'qkv_weight': jax.random.normal(ks[1], (qkv_out, H), jnp.float32) * w_scale, 'proj_weight': jax.random.normal(ks[2], (H, H), jnp.float32) * w_scale, 'router_weight': jax.random.normal(ks[3], (NUM_EXPERTS, H), jnp.float32) * w_scale, 'moe_w1': jax.random.normal(ks[4], (NUM_EXPERTS, H, F), jnp.float32) * w_scale, 'moe_w2': jax.random.normal(ks[5], (NUM_EXPERTS, F, H), jnp.float32) * w_scale}
    _L0_ffn_all = _L0_ffn_setup()
    _L0_ffn_in = {k: v for k, v in _L0_ffn_all.items() if k in ('ln1_weight', 'ln1_bias', 'ln2_weight', 'ln2_bias', 'qkv_weight', 'proj_weight', 'router_weight', 'moe_w1', 'moe_w2')}
    del _L0_ffn_all
    return {'x': x, 'ctx_1024': ctx_1024, 'mask_BxS2_ik0': mask_BxS2_ik0, 'L0_xattn_w_q': _L0_xattn_in['w_q'], 'L0_xattn_w_k': _L0_xattn_in['w_k'], 'L0_xattn_w_v': _L0_xattn_in['w_v'], 'L0_xattn_w_o': _L0_xattn_in['w_o'], 'L0_ffn_ln1_weight': _L0_ffn_in['ln1_weight'], 'L0_ffn_ln1_bias': _L0_ffn_in['ln1_bias'], 'L0_ffn_ln2_weight': _L0_ffn_in['ln2_weight'], 'L0_ffn_ln2_bias': _L0_ffn_in['ln2_bias'], 'L0_ffn_qkv_weight': _L0_ffn_in['qkv_weight'], 'L0_ffn_proj_weight': _L0_ffn_in['proj_weight'], 'L0_ffn_router_weight': _L0_ffn_in['router_weight'], 'L0_ffn_moe_w1': _L0_ffn_in['moe_w1'], 'L0_ffn_moe_w2': _L0_ffn_in['moe_w2']}

def reference(x, ctx_1024, mask_BxS2_ik0, L0_xattn_w_q, L0_xattn_w_k, L0_xattn_w_v, L0_xattn_w_o, L0_ffn_ln1_weight, L0_ffn_ln1_bias, L0_ffn_ln2_weight, L0_ffn_ln2_bias, L0_ffn_qkv_weight, L0_ffn_proj_weight, L0_ffn_router_weight, L0_ffn_moe_w1, L0_ffn_moe_w2):
    import jax
    import jax.numpy as jnp

    def _L0_xattn_ref(q, k, v, mask, w_q, w_k, w_v, w_o):
        import jax, jax.numpy as jnp
        import numpy as np
        B, S, D, H = (4, 512, 256, 16)
        DK = D // H

        def _rope(x):
            s, d = (x.shape[-2], x.shape[-1])
            inv_freq = 1.0 / 10000.0 ** (jnp.arange(0, d, 2, dtype=jnp.float32) / d)
            angles = jnp.arange(s, dtype=jnp.float32)[:, None] * inv_freq[None, :]
            ang = jnp.repeat(angles, 2, axis=-1)
            cos, sin = (jnp.cos(ang), jnp.sin(ang))
            xp = x.reshape(*x.shape[:-1], d // 2, 2)
            rot = jnp.stack((-xp[..., 1], xp[..., 0]), axis=-1).reshape(x.shape)
            return x * cos + rot * sin

        def split_heads(x):
            b, s, _ = x.shape
            return x.reshape(b, s, H, DK).transpose(0, 2, 1, 3)
        query = split_heads(q @ w_q.T)
        key_ = split_heads(k @ w_k.T)
        value = split_heads(v @ w_v.T)
        query = _rope(query)
        key_ = _rope(key_)
        scores = jnp.einsum('bhqd,bhkd->bhqk', query, key_) / np.sqrt(DK)
        scores = jnp.where(mask[:, None, None, :] == 0, -10000.0, scores)
        attn = jax.nn.softmax(scores, axis=-1)
        x = jnp.einsum('bhqk,bhkd->bhqd', attn, value)
        x = x.transpose(0, 2, 1, 3).reshape(q.shape[0], -1, H * DK)
        return x @ w_o.T

    def _L0_ffn_ref(hidden_states, ln1_weight, ln1_bias, ln2_weight, ln2_bias, qkv_weight, proj_weight, router_weight, moe_w1, moe_w2):
        import jax, jax.numpy as jnp
        import numpy as np
        EPS = 1e-05
        NUM_HEADS = 16
        NUM_KV_HEADS = 4
        NUM_EXPERTS = 8
        TOP_K = 2

        def _layernorm(x, w, b):
            mu = jnp.mean(x, axis=-1, keepdims=True)
            var = jnp.mean((x - mu) ** 2, axis=-1, keepdims=True)
            return (x - mu) * jax.lax.rsqrt(var + EPS) * w + b
        S, B, H = hidden_states.shape
        hd = H // NUM_HEADS
        rep = NUM_HEADS // NUM_KV_HEADS
        scale = 1.0 / hd ** 0.5
        ln1_out = _layernorm(hidden_states, ln1_weight, ln1_bias)
        qkv = jnp.einsum('sbh,oh->sbo', ln1_out, qkv_weight)
        q = qkv[..., :NUM_HEADS * hd].reshape(S, B, NUM_HEADS, hd)
        k = qkv[..., NUM_HEADS * hd:(NUM_HEADS + NUM_KV_HEADS) * hd].reshape(S, B, NUM_KV_HEADS, hd)
        v = qkv[..., (NUM_HEADS + NUM_KV_HEADS) * hd:].reshape(S, B, NUM_KV_HEADS, hd)
        k = jnp.repeat(k, rep, axis=2)
        v = jnp.repeat(v, rep, axis=2)
        scores = jnp.einsum('sbhd,tbhd->bhst', q, k) * scale
        causal = jnp.tril(jnp.ones((S, S), bool))
        scores = jnp.where(causal, scores, jnp.finfo(scores.dtype).min)
        probs = jax.nn.softmax(scores, axis=-1)
        attn = jnp.einsum('bhst,tbhd->sbhd', probs, v).reshape(S, B, H)
        proj_out = jnp.einsum('sbh,oh->sbo', attn, proj_weight)
        hidden_after_attn = hidden_states + proj_out
        ln2_out = _layernorm(hidden_after_attn, ln2_weight, ln2_bias)
        x = ln2_out.reshape(-1, H)
        logits = jnp.einsum('th,eh->te', x, router_weight)
        gate = jax.nn.softmax(logits, axis=-1)
        top_probs, top_idx = jax.lax.top_k(gate, TOP_K)
        h_mid = jax.nn.gelu(jnp.einsum('th,ehf->etf', x, moe_w1))
        expert_out = jnp.einsum('etf,efh->eth', h_mid, moe_w2)
        e_ids = jnp.arange(NUM_EXPERTS)[:, None, None]
        weights = jnp.sum(jnp.where(top_idx[None] == e_ids, top_probs[None], 0.0), axis=-1)
        moe_out = jnp.einsum('eth,et->th', expert_out, weights).reshape(S, B, H)
        return hidden_after_attn + moe_out
    x = x + _L0_xattn_ref(_layernorm(x, axis=-1), ctx_1024, ctx_1024, mask_BxS2_ik0, L0_xattn_w_q, L0_xattn_w_k, L0_xattn_w_v, L0_xattn_w_o)
    x = x + _L0_ffn_ref(_layernorm(x, axis=-1), L0_ffn_ln1_weight, L0_ffn_ln1_bias, L0_ffn_ln2_weight, L0_ffn_ln2_bias, L0_ffn_qkv_weight, L0_ffn_proj_weight, L0_ffn_router_weight, L0_ffn_moe_w1, L0_ffn_moe_w2)
    return x

_drawn_inputs = setup_inputs


def setup_inputs(seed=0):
    import zlib

    import numpy as np

    out = dict(_drawn_inputs(seed))
    spreads = {'L0_ffn_ln1_weight': (1.0, 0.6),
     'L0_ffn_ln1_bias': (0.0, 0.8),
     'L0_ffn_ln2_weight': (1.0, 0.6),
     'L0_ffn_ln2_bias': (0.0, 0.8)}
    factors = {'L0_ffn_router_weight': 6.762, 'L0_ffn_moe_w1': 6.035, 'L0_ffn_moe_w2': 5.846}
    for name, (base, spread) in spreads.items():
        noise = np.random.default_rng([zlib.crc32(name.encode()), seed]).standard_normal(out[name].shape)
        drawn = base * np.exp(spread * noise) if base else spread * noise
        out[name] = jnp.asarray(drawn.astype(out[name].dtype))
    for name, factor in factors.items():
        out[name] = (out[name] * factor).astype(out[name].dtype)
    return out
```

```python
import numpy as np
import concourse.bass as bass
from concourse import mybir
from contextlib import ExitStack

F32 = mybir.dt.float32
F32R = mybir.dt.float32r
BF16 = mybir.dt.bfloat16
I32 = mybir.dt.int32
ALU = mybir.AluOpType
ACT = mybir.ActivationFunctionType
AX = mybir.AxisListType

P = 128
B, SQ, SK, D = 4, 512, 1024, 256
H, DK = 16, 16
KC = D // P
QT, KT = SQ // P, SK // P
NT = B * QT
EPS = 1e-5
MASKED = -10000.0
HH = H // 2
UNITS = 2 * B
Q_PIECES = (0, 0, 1, 1, 0, 2)
K_PIECES = (0, 1, 0, 1, 2, 0)
R_MASK = len(Q_PIECES) * DK
R_MAX = R_MASK + 2
R_ALL = R_MAX + 3
MASK_PARTS = (-39936.0, -64.0)
assert sum(MASK_PARTS) == MASKED * DK ** 0.5


def attention_jobs():
    def proj(b):
        jobs = [("xT", b)] + [("q", b, j) for j in range(QT)] + [("trq", b)]
        for g in range(2):
            jobs += [("kv", b, g * 4 + j) for j in range(4)] + [("trk", b, g)]
        return jobs

    def maxes(u):
        return [("max", u, h, qt) for qt in range(QT) for h in range(HH)]

    cost = {"xT": 1.2, "q": .85, "kv": 1.3, "trq": 1.2, "trk": 1.2, "max": 1.13, "mxt": .7,
            "out": .8, "oT": 1.2, "oP": 2.6}
    before = proj(0) + maxes(0) + [("mxt", 0)]
    places = []
    for u in range(UNITS):
        b, c = divmod(u, 2)
        work = []
        if c == 0:
            m = maxes(u + 1)
            work = m[:16] + (proj(b + 1) if b + 1 < B else []) + m[16:] + [("mxt", u + 1)]
        elif b + 1 < B:
            work = maxes(u + 1) + [("mxt", u + 1)]
        total, spent, i = sum(cost[j[0]] for j in work), 0.0, 0
        for g in range(16):
            now = []
            G = 16 * u + g
            if g % 8 == 1 and G > 8:
                now.append(("out", G // 8 - 1))
            if g == 3 and c == 0 and b > 0:
                now.append(("oT", b - 1))
            if g == 4 and c == 0 and b > 0:
                now.append(("oP", b - 1))
            while i < len(work) and spent < total * (g + 1) / 15.5:
                now.append(work[i])
                spent += cost[work[i][0]]
                i += 1
            places.append(now)
        places[-1] += work[i:]
    after = [("out", 2 * UNITS - 1), ("oT", B - 1), ("oP", B - 1)]
    jobs = before + [j for now in places for j in now] + after
    index = {j: n for n, j in enumerate(jobs)}
    return index, before, places, after


def cross_attention(nc, ctx, io, xt, wide, narrow, values):
    index, before, places, after = attention_jobs()
    jobs = sorted(index, key=index.get)

    def sb(name, shape, dt):
        return ctx.enter_context(nc.sbuf_tensor(name, shape, dt))

    def sem(name):
        return ctx.enter_context(nc.semaphore(name))

    ident = sb("ident", [P, P], F32)
    w_hi = {w: sb(f"w{w}_hi", [P, KC, D], F32R) for w in "qkvo"}
    w_lo = {w: sb(f"w{w}_lo", [P, KC, D], F32R) for w in "qkvo"}
    cos = sb("cos", [P, KT, DK], F32)
    sin = sb("sin", [P, KT, DK], F32)
    mcol_i = sb("mcol_i", [P, B * KT], I32)
    mcol = sb("mcol", [P, B * KT], F32)
    kcos = sb("kcos", [P, 2, KT, DK], F32)
    ksin = sb("ksin", [P, 2, KT, DK], F32)
    mcoef = sb("mcoef", [2 * B, 1], F32)
    mrow = sb("mrow", [2 * B, SK], BF16)
    ones = sb("ones", [8, 512], BF16)
    stats = sb("stats", [P, NT, 6], F32)
    mv = sb("mv", [P, NT, 2], F32)
    varc = sb("varc", [P, NT], F32)
    std = sb("std", [P, NT], F32)
    rstd = sb("rstd", [P, NT], F32)
    xT_hi = sb("xT_hi", [P, KC, SQ], F32R)
    xT_lo = sb("xT_lo", [P, KC, SQ], F32R)
    craw = sb("craw", [P, KC, 512], F32)
    c_hi = sb("c_hi", [P, KC, SK], F32R)
    c_lo = sb("c_lo", [P, KC, SK], F32R)
    rope_b = sb("rope_b", [P, 2, D], F32)
    roped = sb("roped", [P, 8, D], F32)
    pieces = sb("pieces", [P, 2, 3, KC, 512], BF16)
    rest = sb("rest", [P, KC, 512], F32)
    wraw = rest[:, :, 0:D]
    qst = [sb(f"qst{i}", [R_ALL, HH, SQ], BF16) for i in range(3)]
    kst = [sb(f"kst{i}", [R_ALL, HH, SK], BF16) for i in range(3)]
    mx = [sb(f"mx{i}", [P, QT * HH], F32) for i in range(2)]
    mxp = sb("mxp", [HH, 3, SQ], BF16)
    vaug = [sb(f"vaug{i}", [P, KT, H, DK + 1], F32) for i in range(2)]
    NP = 8
    probs = sb("probs", [P, NP, SQ], F32)
    mrow_i = probs[0:2 * B, 0:2, :].rearrange("r a n -> r (a n)").bitcast(I32)
    outT = sb("outT", [P, SQ], F32)
    rec = sb("rec", [P, 16], F32)
    attn = sb("attn", [P, QT, D], F32)
    xn = attn
    aT_hi, aT_lo = xT_hi, xT_lo
    q_dram = nc.dram_tensor("q_pieces", [B, KC, 3, P, SQ], BF16, kind="Internal").ap()
    m_dram = nc.dram_tensor("m_pieces", [UNITS, HH, 3, SQ], BF16, kind="Internal").ap()
    k_dram = nc.dram_tensor("k_pieces", [B, KC, 3, P, SK], BF16, kind="Internal").ap()

    x_in = [sem(f"x_in{b}") for b in range(B)]
    w_in, tab_in, c_in = sem("w_in"), sem("tab_in"), sem("c_in")
    ones_set, ones_in = sem("ones_set"), sem("ones_in")
    stack_in = [sem(f"stack_in{i}") for i in range(3)]
    maxrow_in, maxrow_out = sem("maxrow_in"), sem("maxrow_out")
    pieces_out = [sem(f"pieces_out{i}") for i in range(2)]
    w_split, c_split, mask_set = sem("w_split"), sem("c_split"), sem("mask_set")
    var_set, std_set, xn_set, values_prepared = sem("var_set"), sem("std_set"), sem("xn_set"), sem("values_prepared")
    dve_step, pool_step = sem("dve_step"), sem("pool_step")
    pe_done, dve_done, act_done, pool_done = sem("pe_done"), sem("dve_done"), sem("act_done"), sem("pool_done")
    score_ready, exp_done, pv_done, outT_set = sem("score_ready"), sem("exp_done"), sem("pv_done"), sem("outT_set")

    STACK = 16 * (len(Q_PIECES) + len(K_PIECES) + 1)
    SPLIT = ("xT", "trq", "trk", "mxt", "oT")
    ACT_KINDS = SPLIT + ("kv",)
    POOL_KINDS = ("q", "kv", "trq", "trk", "mxt")
    PIECED = ("trq", "trk", "mxt")

    def act_count(n):
        return sum(j[0] in ACT_KINDS for j in jobs[:n + 1])

    def pool_count(n):
        return sum(j[0] in POOL_KINDS for j in jobs[:n + 1])

    def last_before(n, kinds):
        return max((m for m in range(n) if jobs[m][0] in kinds), default=-1)

    def tile_number(j):
        return j[1] * (QT + KT) + (j[2] if j[0] == "q" else QT + j[2])

    def transposed_by(tile):
        b, r = divmod(tile, QT + KT)
        return index[("trq", b) if r < QT else ("trk", b, (r - QT) // 4)]

    def piece_job(j):
        return 3 * j[1] + (0 if j[0] == "trq" else 1 + j[2])

    def pieces_stored(last, i):
        return sum(t % 2 == i for t in range(last + 1))

    block = ctx.enter_context(nc.Block())

    @block.sync
    def _(sp):
        for b in range(B):
            sp.dma_start(xt[:, QT * b:QT * b + QT, :],
                         io["x"][SQ * b:SQ * b + SQ, :].rearrange("(t p) d -> p t d", p=P)).then_inc(x_in[b], 16)
        for dst, name in ((ident[:, :], "ident"), (mcol_i[:, :], "mask_col"), (mrow_i, "mask_row"), (mcoef[:, :], "mask_coef")):
            sp.dma_start(dst, io[name]).then_inc(tab_in, 16)
        sp.dma_start(cos[:, :, :], io["cos"]).then_inc(tab_in, 16)
        sp.dma_start(sin[:, :, :], io["sin"]).then_inc(tab_in, 16)
        def load_context(i):
            if i > 0:
                sp.wait_ge(c_split, i)
            sp.dma_start(craw[:, :, :], io["ctxT"][:, 512 * i:512 * i + 512].rearrange("(k p) t -> p k t", p=P)).then_inc(c_in, 16)

        load_context(0)
        sp.wait_ge(ones_set, 1)
        for i in range(3):
            for st, n in ((qst[i], HH), (kst[i], 2 * HH)):
                sp.dma_start(st[R_MASK:R_ALL, :, :].rearrange("r h (a n) -> r (h a) n", n=512),
                             ones[0:R_ALL - R_MASK, :].unsqueeze(1).to_broadcast([R_ALL - R_MASK, n, 512])).then_inc(ones_in, 16)
        sp.wait_ge(ones_in, 6 * 16)
        sp.wait_ge(mask_set, 1)

        def load_stack(u):
            b, c = divmod(u, 2)
            if u >= 3:
                sp.wait_ge(score_ready, 64 * (u - 2))
            for g in range(len(Q_PIECES)):
                rows = slice(DK * g, DK * g + DK)
                sp.dma_start(qst[u % 3][rows, :, :],
                             q_dram[b, c, Q_PIECES[g]].rearrange("(h d) t -> d h t", h=HH)).then_inc(stack_in[u % 3], 16)
                sp.dma_start(kst[u % 3][rows, :, :],
                             k_dram[b, c, K_PIECES[g]].rearrange("(h d) t -> d h t", h=HH)).then_inc(stack_in[u % 3], 16)
            sp.dma_start(kst[u % 3][R_MASK:R_MAX, :, :],
                         mrow[2 * b:2 * b + 2, :].unsqueeze(1).to_broadcast([2, HH, SK])).then_inc(stack_in[u % 3], 16)

        def load_max_rows(u):
            sp.wait_ge(pool_done, pool_count(index[("mxt", u)]))
            sp.dma_start(m_dram[u], mxp[:, :, :]).then_inc(maxrow_out, 16)
            sp.wait_ge(maxrow_out, 16 * (u + 1))
            sp.dma_start(qst[u % 3][R_MAX:R_ALL, :, :], m_dram[u].rearrange("h a t -> a h t")).then_inc(maxrow_in, 16)

        def store_pieces(j):
            sp.wait_ge(pool_done, pool_count(index[j]))
            for c in range(KC):
                if j[0] == "trq":
                    dst = q_dram[j[1], c]
                else:
                    dst = k_dram[j[1], c][:, :, 512 * j[2]:512 * j[2] + 512]
                sp.dma_start(dst.rearrange("a p t -> p a t"), pieces[:, piece_job(j) % 2, :, c, :]).then_inc(pieces_out[piece_job(j) % 2], 16)

        load_context(1)
        for b in range(B):
            store_pieces(("trq", b))
            store_pieces(("trk", b, 0))
            if b + 1 < B:
                load_context(2 * b + 2)
            store_pieces(("trk", b, 1))
            if b + 1 < B:
                load_context(2 * b + 3)
            for i in range(2):
                sp.wait_ge(pieces_out[i], 32 * pieces_stored(3 * b + 2, i))
            load_stack(2 * b)
            if b > 0:
                load_max_rows(2 * b - 1)
            load_stack(2 * b + 1)
            load_max_rows(2 * b)
        load_max_rows(UNITS - 1)

    @block.gpsimd
    def _(pool):
        steps = [0]

        def step(ins):
            steps[0] += 1
            ins.then_inc(pool_step, 1)
            pool.wait_ge(pool_step, steps[0])

        nc.gpsimd.memset(ones[:, :], 1.0).then_inc(ones_set, 1)

        def split_context(i):
            b, g = divmod(i, 2)
            part = slice(512 * g, 512 * g + 512)
            pool.wait_ge(c_in, 16 * (i + 1))
            if b > 0:
                pool.wait_ge(pe_done, index[("kv", b - 1, 4 * g + 3)] + 1)
            step(nc.gpsimd.tensor_copy(c_hi[:, :, part], craw[:, :, :]))
            nc.gpsimd.tensor_tensor(c_lo[:, :, part], craw[:, :, :], c_hi[:, :, part].bitcast(F32), ALU.subtract).then_inc(c_split, 1)

        split_context(0)
        split_context(1)
        for i in range(2):
            nc.gpsimd.memset(vaug[i][:, :, :, DK:DK + 1], 1.0).then_inc(values_prepared, 1)

        def job(j):
            n, kind = index[j], j[0]
            if kind not in POOL_KINDS:
                return
            pool.wait_ge(dve_done, n + 1)
            if kind in ("q", "kv"):
                r = tile_number(j)
                nc.gpsimd.tensor_tensor(roped[:, r % 8, :], roped[:, r % 8, :], rope_b[:, r % 2, :], ALU.add).then_inc(pool_done, 1)
                return
            if kind == "mxt":
                mid, low, r1 = mxp[:, 1, :], mxp[:, 2, :], rest[0:HH, 0, :]
            else:
                i = piece_job(j) % 2
                mid, low, r1 = pieces[:, i, 1, :, :], pieces[:, i, 2, :, :], rest[:, :, :]
            step(nc.gpsimd.tensor_copy(mid, r1))
            nc.gpsimd.tensor_tensor(low, r1, mid, ALU.subtract).then_inc(pool_done, 1)
            if kind == "trk" and j[1] + 1 < B:
                split_context(2 * (j[1] + 1) + j[2])

        for j in before:
            job(j)
        for g in range(16 * UNITS):
            for j in places[g]:
                job(j)

    @block.scalar
    def _(act):
        for n, w in enumerate("qkvo"):
            if n >= 1:
                act.wait_ge(w_split, n)
            act.dma_start(wraw, io["w" + w].rearrange("(k p) n -> p k n", p=P)).then_inc(w_in, 16)
            if n == 0:
                act.wait_ge(var_set, 1)
                nc.scalar.activation(std[:, :], varc[:, :], ACT.Sqrt).then_inc(std_set, 1)

        def job(j):
            n, kind = index[j], j[0]
            if kind not in ACT_KINDS:
                return
            act.wait_ge(pe_done, n + 1)
            src = wide[n % 2]
            if kind == "kv":
                b, kt = j[1:]
                if kt == 0:
                    if b < 2:
                        act.wait_ge(values_prepared, 3)
                    else:
                        act.wait_ge(pv_done, 32 * (b - 1))
                nc.scalar.activation(vaug[b % 2][:, kt, :, 0:DK],
                                     src[:, 1, 0:D].rearrange("p (h d) -> p h d", h=H), ACT.Copy).then_inc(act_done, 1)
                return
            if kind in ("xT", "oT"):
                m = last_before(n, ("q", "oP"))
                if m >= 0:
                    act.wait_ge(pe_done, m + 1)
                dst, src = xT_hi[:, :, :], src[:, :, :]
            elif kind in ("trq", "trk"):
                if piece_job(j) >= 2:
                    act.wait_ge(pieces_out[piece_job(j) % 2], 32 * (piece_job(j) // 2))
                dst, src = pieces[:, piece_job(j) % 2, 0, :, :], src[:, :, :]
            else:
                if j[1] > 0:
                    act.wait_ge(maxrow_out, 16 * j[1])
                dst, src = mxp[:, 0, :], src[0:HH, 0, :]
            nc.scalar.activation(dst, src, ACT.Copy).then_inc(act_done, 1)

        def take_out(quad):
            act.wait_ge(pv_done, 8 * (quad + 1))
            if quad >= 1:
                act.wait_ge(pe_done, index[("out", quad - 1)] + 1)
            nc.scalar.activation(outT[:, :], values[:, :], ACT.Copy).then_inc(outT_set, 1)

        for j in before:
            job(j)
        for g in range(16 * UNITS):
            for hq in range(4):
                n = 4 * g + hq
                act.wait_ge(score_ready, n + 1)
                if n >= NP:
                    act.wait_ge(pv_done, (n - NP) // 4 + 1)
                nc.scalar.activation(probs[:, n % NP, :], narrow[n % 3][:, :], ACT.Exp, scale=DK ** -0.5).then_inc(exp_done, 1)
            if g % 8 == 0 and g > 0:
                take_out(g // 8 - 1)
            for j in places[g]:
                job(j)
        take_out(2 * UNITS - 1)
        for j in after:
            job(j)

    @block.vector
    def _(dve):
        steps = [0]

        def step(ins):
            steps[0] += 1
            ins.then_inc(dve_step, 1)

        def settle():
            dve.wait_ge(dve_step, steps[0])

        nc.vector.memset(values[:, :], 0.0).then_inc(values_prepared, 1)
        for b in range(B):
            dve.wait_ge(x_in[b], 16)
            for t in range(QT * b, QT * b + QT):
                step(nc.vector.bn_stats(stats[:, t, :], xt[:, t, :]))
        settle()
        for t in range(NT):
            step(nc.vector.bn_aggr(mv[:, t, :], stats[:, t, :]))
        settle()
        nc.vector.tensor_scalar_add(varc[:, :], mv[:, :, 1], EPS).then_inc(var_set, 1)
        for n, w in enumerate("qkvo"):
            dve.wait_ge(w_in, 16 * (n + 1))
            step(nc.vector.tensor_copy(w_hi[w][:, :, :], wraw))
            settle()
            nc.vector.tensor_tensor(w_lo[w][:, :, :], wraw, w_hi[w][:, :, :].bitcast(F32), ALU.subtract).then_inc(w_split, 1)
        dve.wait_ge(tab_in, 96)
        step(nc.vector.tensor_scalar(mcol[:, :], mcol_i[:, :], 0.0, None, ALU.not_equal))
        nc.vector.tensor_scalar(mrow[:, :], mrow_i, 0.0, mcoef[:, 0:1], ALU.is_equal, ALU.mult).then_inc(mask_set, 1)
        settle()
        def key_tables(b):
            for out, table in ((kcos, cos), (ksin, sin)):
                step(nc.vector.tensor_tensor(out[:, b % 2, :, :], table[:, :, :],
                                             mcol[:, KT * b:KT * b + KT].unsqueeze(2).to_broadcast([P, KT, DK]), ALU.mult))

        key_tables(0)
        dve.wait_ge(std_set, 1)
        step(nc.vector.reciprocal(rstd[:, :], std[:, :]))
        settle()

        def normalise(b):
            for t in range(QT):
                nc.vector.tensor_scalar(xn[:, t, :], xt[:, QT * b + t, :], mv[:, QT * b + t, 0:1],
                                        rstd[:, QT * b + t:QT * b + t + 1], ALU.subtract, ALU.mult).then_inc(xn_set, 1)

        normalise(0)

        def job(j):
            n, kind = index[j], j[0]
            slot = wide[n % 2]
            dve.wait_ge(pe_done, n + 1)
            if kind in SPLIT:
                dve.wait_ge(act_done, act_count(n))
            if kind in PIECED:
                m = last_before(n, PIECED)
                if m >= 0:
                    dve.wait_ge(pool_done, pool_count(m))
            if kind in ("xT", "oT"):
                nc.vector.tensor_tensor(xT_lo[:, :, :], slot[:, :, :], xT_hi[:, :, :].bitcast(F32), ALU.subtract).then_inc(dve_done, 1)
                if kind == "xT" and j[1] + 1 < B:
                    key_tables(j[1] + 1)
                if j == ("xT", 0):
                    normalise(1)
                elif kind == "oT" and j[1] + 2 < B:
                    normalise(j[1] + 2)
            elif kind in ("q", "kv"):
                r = tile_number(j)
                if r >= 2:
                    before_last = [m for m in range(n) if jobs[m][0] in ("q", "kv")][-2]
                    dve.wait_ge(pool_done, pool_count(before_last))
                    if r >= 8:
                        dve.wait_ge(pe_done, transposed_by(r - 8) + 1)
                if kind == "q":
                    c, s = cos[:, j[2], :], sin[:, j[2], :]
                else:
                    c, s = kcos[:, j[1] % 2, j[2], :], ksin[:, j[1] % 2, j[2], :]
                    if j[2] == 0:
                        settle()
                a = roped[:, r % 8, :].rearrange("p (h d) -> p h d", h=H)
                rot = rope_b[:, r % 2, :].rearrange("p (h i two) -> p h i two", h=H, two=2)
                swapped = slot[:, 0, 0:D].rearrange("p (h i two) -> p h i two", h=H, two=2)[:, :, :, ::-1]
                nc.vector.tensor_tensor(a, slot[:, 0, 0:D].rearrange("p (h d) -> p h d", h=H),
                                        c.unsqueeze(1).to_broadcast([P, H, DK]), ALU.mult)
                nc.vector.tensor_tensor(rot, swapped, s.rearrange("p (i two) -> p i two", two=2)
                                        .unsqueeze(1).to_broadcast([P, H, DK // 2, 2]), ALU.mult).then_inc(dve_done, 1)
            elif kind in ("trq", "trk"):
                nc.vector.tensor_tensor(rest[:, :, :], slot[:, :, :], pieces[:, piece_job(j) % 2, 0, :, :], ALU.subtract).then_inc(dve_done, 1)
            elif kind == "mxt":
                nc.vector.tensor_tensor(rest[0:HH, 0, :], slot[0:HH, 0, :], mxp[:, 0, :], ALU.subtract).then_inc(dve_done, 1)
            elif kind == "max":
                u, h, qt = j[1:]
                if u >= 2 and h == 0 and qt == 0:
                    dve.wait_ge(pe_done, index[("mxt", u - 2)] + 1)
                nc.vector.tensor_reduce(mx[u % 2][:, HH * qt + h:HH * qt + h + 1], slot[:, :, :], axis=AX.XY, op=ALU.max,
                                        negate=True).then_inc(dve_done, 1)
            elif kind == "out":
                b, first = j[1] // 4, 64 * (j[1] % 4)
                if b > 0 and first == 0:
                    dve.wait_ge(pe_done, index[("oT", b - 1)] + 1)
                if j[1] > 0:
                    dve.wait_ge(dve_done, index[("out", j[1] - 1)] + 1)
                o = slot[:, 0, :].rearrange("p (q h e) -> p q h e", q=QT, e=32)
                step(nc.vector.reciprocal(rec[:, :].rearrange("p (q h e) -> p q h e", q=QT, e=1), o[:, :, :, DK:DK + 1]))
                settle()
                nc.vector.tensor_tensor(attn[:, :, first:first + 64].rearrange("p q (h d) -> p q h d", d=DK), o[:, :, :, 0:DK],
                                        rec[:, :].rearrange("p (q h e) -> p q h e", q=QT, e=1).to_broadcast([P, QT, 4, DK]),
                                        ALU.mult).then_inc(dve_done, 1)
            elif kind == "oP":
                b = j[1]
                xb = xt[:, QT * b:QT * b + QT, :]
                nc.vector.tensor_tensor(xb, slot[:, :, :].rearrange("p k (t d) -> p (k t) d", d=D), xb, ALU.add).then_inc(dve_done, 1)

        for j in before:
            job(j)
        for g in range(16 * UNITS):
            for j in places[g]:
                job(j)
        for j in after:
            job(j)

    @block.tensor
    def _(pe):
        pe.wait_ge(tab_in, 96)
        pe.wait_ge(values_prepared, 3)

        def project(out, hi, lo, t, w, cols=slice(0, D)):
            for i, (a, c) in enumerate(((hi, w_hi[w]), (hi, w_lo[w]), (lo, w_hi[w]))):
                for k in range(KC):
                    last = nc.tensor.matmul(out, a[:, k, P * t:P * t + P], c[:, k, cols],
                                            start=(i, k) == (0, 0), stop=(i, k) == (2, KC - 1))
            return last

        def job(j):
            n, kind = index[j], j[0]
            slot = wide[n % 2]
            if n >= 2:
                pe.wait_ge(dve_done, n - 1)
                if jobs[n - 2][0] == "kv":
                    pe.wait_ge(act_done, act_count(n - 2))
            if kind == "xT":
                pe.wait_ge(xn_set, QT * (j[1] + 1))
                for k in range(KC):
                    for t in range(QT):
                        last = nc.tensor.transpose(slot[:, k, P * t:P * t + P], xn[:, t, P * k:P * k + P], ident[:, :])
            elif kind == "q":
                if j[2] == 0:
                    m = index[("xT", j[1])]
                    pe.wait_ge(dve_done, m + 1)
                    pe.wait_ge(w_split, 1)
                last = project(slot[:, 0, 0:D], xT_hi, xT_lo, j[2], "q")
            elif kind == "kv":
                if j[2] == 0:
                    pe.wait_ge(c_split, j[1] + 1)
                    pe.wait_ge(w_split, 3)
                project(slot[:, 0, 0:D], c_hi, c_lo, j[2], "k")
                last = project(slot[:, 1, 0:D], c_hi, c_lo, j[2], "v")
            elif kind in ("trq", "trk"):
                b = j[1]
                first = (QT + KT) * b + (0 if kind == "trq" else QT + 4 * j[2])
                pe.wait_ge(pool_done, pool_count(last_before(n, ("q", "kv"))))
                for k in range(KC):
                    for t in range(4):
                        last = nc.tensor.transpose(slot[:, k, P * t:P * t + P], roped[:, (first + t) % 8, P * k:P * k + P], ident[:, :])
            elif kind == "max":
                u, h, qt = j[1:]
                if h == 0 and qt == 0:
                    pe.wait_ge(stack_in[u % 3], STACK * (u // 3 + 1))
                for k in range(2):
                    last = nc.tensor.matmul(slot[:, k, :], qst[u % 3][0:R_MAX, h, P * qt:P * qt + P],
                                            kst[u % 3][0:R_MAX, h, 512 * k:512 * k + 512], start=True, stop=True)
            elif kind == "mxt":
                pe.wait_ge(dve_done, n)
                for qt in range(QT):
                    last = nc.tensor.transpose(slot[0:HH, 0, P * qt:P * qt + P], mx[j[1] % 2][:, HH * qt:HH * qt + HH], ident[:, :])
            elif kind == "out":
                pe.wait_ge(outT_set, j[1] + 1)
                for qt in range(QT):
                    last = nc.tensor.transpose(slot[:, 0, P * qt:P * qt + P], outT[:, P * qt:P * qt + P], ident[:, :])
            elif kind == "oT":
                pe.wait_ge(dve_done, index[("out", 4 * j[1] + 3)] + 1)
                for k in range(KC):
                    for t in range(QT):
                        last = nc.tensor.transpose(slot[:, k, P * t:P * t + P], attn[:, t, P * k:P * k + P], ident[:, :])
            elif kind == "oP":
                pe.wait_ge(dve_done, index[("oT", j[1])] + 1)
                pe.wait_ge(w_split, 4)
                for t in range(QT):
                    last = project(slot[:, t // 2, D * (t % 2):D * (t % 2) + D], aT_hi, aT_lo, t, "o")
            last.then_inc(pe_done, 1)

        def scores(g):
            u, quad, kt = g // 16, g // 8 % 2, g % 8
            if g % 16 == 0:
                pe.wait_ge(maxrow_in, 16 * (u + 1))
            for hq in range(4):
                n, h = 4 * g + hq, 4 * quad + hq
                if n >= 3:
                    pe.wait_ge(exp_done, n - 2)
                nc.tensor.matmul(narrow[n % 3][:, :], kst[u % 3][0:R_ALL, h, P * kt:P * kt + P],
                                 qst[u % 3][0:R_ALL, h, :], start=True, stop=True).then_inc(score_ready, 1)

        def weigh(g):
            b, kt = g // 32, g % 8
            pe.wait_ge(exp_done, 4 * g + 4)
            if g % 32 == 0:
                pe.wait_ge(act_done, act_count(index[("kv", b, KT - 1)]))
            if kt == 0 and g > 0:
                pe.wait_ge(outT_set, g // 8)
            for hq in range(4):
                h = 4 * (g // 8 % 4) + hq
                last = nc.tensor.matmul(values[32 * hq:32 * hq + DK + 1, :], vaug[b % 2][:, kt, h, :], probs[:, (4 * g + hq) % NP, :],
                                        start=kt == 0, stop=kt == KT - 1)
            last.then_inc(pv_done, 1)

        for j in before:
            job(j)
        for g in range(16 * UNITS):
            scores(g)
            if g >= 1:
                weigh(g - 1)
            for j in places[g]:
                job(j)
        weigh(16 * UNITS - 1)
        for j in after:
            job(j)


E_, F, EH = 8, 512, 4
FC = F // P
REP = H // EH
QKV = D + 2 * EH * DK
LEAST = -3.4028234663852886e38


def expert_weights(nc, ctx, io):
    def sb(name, shape, dt):
        return ctx.enter_context(nc.sbuf_tensor(name, shape, dt))

    class Weights:
        raw1, raw2 = sb("raw1", [P, KC, F], F32), sb("raw2", [P, FC, D], F32)
        w1_hi = [sb(f"w1_hi{i}", [P, KC, F], F32R) for i in range(2)]
        w1_lo = [sb(f"w1_lo{i}", [P, KC, F], F32R) for i in range(2)]
        w2_hi = [sb(f"w2_hi{i}", [P, FC, D], F32R) for i in range(2)]
        w2_lo = [sb(f"w2_lo{i}", [P, FC, D], F32R) for i in range(2)]
        arrived = ctx.enter_context(nc.semaphore("expert_arrived"))
        split = ctx.enter_context(nc.semaphore("expert_split"))
        step = ctx.enter_context(nc.semaphore("expert_step"))
    return Weights


def load_expert(sp, nc, W, io, e):
    if e > 0:
        sp.wait_ge(W.split, e)
    sp.dma_start(W.raw1[:, :, :], io["w1"][e].rearrange("(k p) f -> p k f", p=P)).then_inc(W.arrived, 16)
    sp.dma_start(W.raw2[:, :, :], io["w2"][e].rearrange("(k p) d -> p k d", p=P)).then_inc(W.arrived, 16)


def split_expert(pool, nc, W, e):
    i = e % 2
    pool.wait_ge(W.arrived, 32 * (e + 1))
    nc.gpsimd.tensor_copy(W.w1_hi[i][:, :, :], W.raw1[:, :, :]).then_inc(W.step, 1)
    nc.gpsimd.tensor_copy(W.w2_hi[i][:, :, :], W.raw2[:, :, :]).then_inc(W.step, 1)
    pool.wait_ge(W.step, 2 * (e + 1))
    nc.gpsimd.tensor_tensor(W.w1_lo[i][:, :, :], W.raw1[:, :, :], W.w1_hi[i][:, :, :].bitcast(F32), ALU.subtract)
    nc.gpsimd.tensor_tensor(W.w2_lo[i][:, :, :], W.raw2[:, :, :], W.w2_hi[i][:, :, :].bitcast(F32), ALU.subtract).then_inc(W.split, 1)


def attention_and_router(nc, ctx, io, xt, y2_hi, y2_lo, gates, W, wide, narrow, values):
    def sb(name, shape, dt):
        return ctx.enter_context(nc.sbuf_tensor(name, shape, dt))

    def sem(name):
        return ctx.enter_context(nc.semaphore(name))

    ident = sb("ident2", [P, P], F32)
    wraw = sb("wraw2", [P, KC, QKV], F32)
    qkvw_hi, qkvw_lo = sb("qkvw_hi", [P, KC, QKV], F32R), sb("qkvw_lo", [P, KC, QKV], F32R)
    projw_hi, projw_lo = sb("projw_hi", [P, KC, D], F32R), sb("projw_lo", [P, KC, D], F32R)
    rw_hi, rw_lo = sb("rw_hi", [P, KC, E_], F32R), sb("rw_lo", [P, KC, E_], F32R)
    lncol = sb("lncol", [P, 4, KC], F32)
    iota = sb("iota", [P, E_], F32)
    stats, mv = sb("stats2", [P, NT, 6], F32), sb("mv2", [P, NT, 2], F32)
    varc, std, rstd = sb("varc2", [P, NT], F32), sb("std2", [P, NT], F32), sb("rstd2", [P, NT], F32)
    h0 = sb("h0", [P, NT, D], F32)
    norm = sb("norm", [P, 2, QT, D], F32)
    full = sb("full", [P, KC, 512], F32)
    yT_hi, yT_lo = sb("yT_hi", [P, KC, 512], F32R), sb("yT_lo", [P, KC, 512], F32R)
    qkv = sb("qkv", [P, NT, QKV], F32)
    prod = sb("prod", [P, B, D], F32)
    sc = sb("sc", [P, QT * B, B, H], F32)
    top = sb("top", [P, QT * B * H], F32)
    den = sb("den", [P, QT * B * H], F32)
    ao = sb("ao", [P, NT, D], F32)
    logits = sb("logits", [P, NT, E_], F32)
    lmax = sb("lmax", [P, NT], F32)
    gsum = sb("gsum", [P, NT], F32)
    best = sb("best", [P, NT, 8], F32)
    which = sb("which", [P, NT, 8], mybir.dt.uint32)
    chosen = sb("chosen", [P, NT, E_], F32)

    const_in, wraw_in, w_split = sem("const_in2"), sem("wraw_in2"), sem("w_split2")
    var_set, std_set = sem("var_set2"), sem("std_set2")
    norm_set, transposed, full_set, parts_set = sem("norm_set"), sem("transposed"), sem("full_set"), sem("parts_set")
    product_ready, qkv_copied, added = sem("product_ready"), sem("qkv_copied"), sem("added")
    scores_set, exps_set, ao_set = sem("scores_set"), sem("exps_set"), sem("ao_set")
    logits_ready, shifted, gate_exps = sem("logits_ready"), sem("shifted"), sem("gate_exps")
    residual_set = sem("residual_set")
    x2_set = sem("x2_set")
    dve_step = sem("dve_step2")

    def turn_full(turn):
        return 2 * min(turn + 1, 4) + max(0, min(turn + 1 - 4, 4)) + 2 * max(0, turn + 1 - 8)

    block = ctx.enter_context(nc.Block())
    weights = (("wqkv", wraw[:, :, :], qkvw_hi, qkvw_lo), ("wproj", wraw[:, :, 0:D], projw_hi, projw_lo),
               ("router", wraw[:, :, 0:E_], rw_hi, rw_lo))

    @block.sync
    def _(sp):
        sp.dma_start(ident[:, :], io["ident"]).then_inc(const_in, 16)
        sp.dma_start(lncol[:, :, :], io["lncol"]).then_inc(const_in, 16)
        sp.dma_start(iota[:, :], io["iota"]).then_inc(const_in, 16)
        for n, (name, raw, _, _) in enumerate(weights):
            if n > 0:
                sp.wait_ge(w_split, n)
            sp.dma_start(raw, io[name].rearrange("(k p) n -> p k n", p=P)).then_inc(wraw_in, 16)
        for e in range(2):
            load_expert(sp, nc, W, io, e)

    @block.gpsimd
    def _(pool):
        for e in range(2):
            split_expert(pool, nc, W, e)
        pool.wait_ge(x2_set, 1)
        nc.gpsimd.tensor_tensor(xt[:, :, :], xt[:, :, :], h0[:, :, :], ALU.add).then_inc(residual_set, 1)

    @block.scalar
    def _(act):
        def roots(k):
            act.wait_ge(var_set, k + 1)
            nc.scalar.activation(std[:, :], varc[:, :], ACT.Sqrt).then_inc(std_set, 1)

        def apply_affine(turn):
            which_norm = 0 if turn < 4 else 1
            act.wait_ge(transposed, turn + 1)
            if turn > 0:
                act.wait_ge(parts_set, turn)
            for k in range(KC):
                nc.scalar.activation(full[:, k, :], wide[turn % 2][:, k, :], ACT.Identity,
                                     scale=lncol[:, 2 * which_norm, k:k + 1], bias=lncol[:, 2 * which_norm + 1, k:k + 1]).then_inc(full_set, 1)

        roots(0)
        roots(1)
        act.wait_ge(const_in, 48)
        for s in range(B):
            apply_affine(s)
            for t in range(QT):
                i = QT * s + t
                act.wait_ge(product_ready, i + 1)
                nc.scalar.activation(qkv[:, i, :], narrow[i % 3][:, 0:QKV], ACT.Copy).then_inc(qkv_copied, 1)
        act.wait_ge(scores_set, 1)
        nc.scalar.activation(sc[:, :, :, :], sc[:, :, :, :], ACT.Exp, scale=DK ** -0.5).then_inc(exps_set, 1)
        for s in range(B):
            act.wait_ge(transposed, 4 + s + 1)
            if s > 0:
                act.wait_ge(product_ready, NT + QT * s)
            nc.scalar.activation(yT_hi[:, :, :], wide[s % 2][:, :, :], ACT.Copy).then_inc(full_set, 1)
        roots(2)
        for s in range(B):
            apply_affine(8 + s)
        act.wait_ge(shifted, 1)
        nc.scalar.activation(logits[:, :, :], logits[:, :, :], ACT.Exp).then_inc(gate_exps, 1)

    @block.vector
    def _(dve):
        steps = [0]

        def step(ins):
            steps[0] += 1
            ins.then_inc(dve_step, 1)

        def settle():
            dve.wait_ge(dve_step, steps[0])

        def statistics(k, src):
            for t in range(NT):
                step(nc.vector.bn_stats(stats[:, t, :], src[:, t, :]))
            settle()
            for t in range(NT):
                step(nc.vector.bn_aggr(mv[:, t, :], stats[:, t, :]))
            settle()
            nc.vector.tensor_scalar_add(varc[:, :], mv[:, :, 1], EPS).then_inc(var_set, 1)
            dve.wait_ge(std_set, k + 1)
            step(nc.vector.reciprocal(rstd[:, :], std[:, :]))
            settle()

        def normalise(dst, src, t):
            return nc.vector.tensor_scalar(dst, src, mv[:, t, 0:1], rstd[:, t:t + 1], ALU.subtract, ALU.mult)

        def normalise_turn(turn):
            if turn >= 10 or turn in (2, 3):
                dve.wait_ge(transposed, turn - 1)
            for t in range(QT):
                i = QT * (turn % 4) + t
                last = normalise(norm[:, turn % 2, t, :], h0[:, i, :], i)
            last.then_inc(norm_set, 1)

        def split_turn(turn, hi, lo):
            if turn < 8 and turn % 4 > 0:
                dve.wait_ge(product_ready, NT * (turn // 4) + QT * (turn % 4))
            dve.wait_ge(full_set, turn_full(turn))
            step(nc.vector.tensor_copy(hi, full[:, :, :]))
            settle()
            nc.vector.tensor_tensor(lo, full[:, :, :], hi.bitcast(F32), ALU.subtract).then_inc(parts_set, 1)

        for n, (_, raw, hi, lo) in enumerate(weights):
            dve.wait_ge(wraw_in, 16 * (n + 1))
            step(nc.vector.tensor_copy(hi[:, :, :], raw))
            settle()
            nc.vector.tensor_tensor(lo[:, :, :], raw, hi[:, :, :].bitcast(F32), ALU.subtract).then_inc(w_split, 1)
        step(nc.vector.memset(sc[:, :, :, :], LEAST))
        statistics(0, xt)
        for t in range(NT):
            step(normalise(h0[:, t, :], xt[:, t, :], t))
        settle()
        statistics(1, h0)
        normalise_turn(0)
        normalise_turn(1)
        for s in range(B):
            split_turn(s, yT_hi[:, :, :], yT_lo[:, :, :])
            if s + 2 < B:
                normalise_turn(s + 2)

        def head_dims(i, a):
            return qkv[:, i, a:a + D].rearrange("p (g r d) -> p g r d", g=EH, r=REP)

        def shared(i, a):
            return qkv[:, i, a:a + EH * DK].rearrange("p (g r d) -> p g r d", g=EH, r=1).to_broadcast([P, EH, REP, DK])

        dve.wait_ge(qkv_copied, NT)
        for j in range(QT):
            for s in range(B):
                if j + s > 0:
                    settle()
                for t in range(s + 1):
                    step(nc.vector.tensor_tensor(prod[:, t, :].rearrange("p (g r d) -> p g r d", g=EH, r=REP),
                                                 head_dims(QT * s + j, 0), shared(QT * t + j, D), ALU.mult))
                settle()
                step(nc.vector.tensor_reduce(sc[:, B * j + s, 0:s + 1, :], prod[:, 0:s + 1, :].rearrange("p t (h d) -> p t h d", h=H),
                                             axis=AX.X, op=ALU.add))
        settle()
        by_head = sc[:, :, :, :].rearrange("p a t h -> p a h t")
        topv = top[:, :].rearrange("p (a h) -> p a h", h=H)
        denv = den[:, :].rearrange("p (a h) -> p a h", h=H)
        step(nc.vector.tensor_reduce(topv, by_head, axis=AX.X, op=ALU.max))
        settle()
        nc.vector.tensor_tensor(sc[:, :, :, :], sc[:, :, :, :], topv.unsqueeze(2).to_broadcast([P, QT * B, B, H]), ALU.subtract).then_inc(scores_set, 1)
        dve.wait_ge(exps_set, 1)
        step(nc.vector.tensor_reduce(denv, by_head, axis=AX.X, op=ALU.add))
        settle()
        step(nc.vector.reciprocal(top[:, :], den[:, :]))
        settle()
        step(nc.vector.tensor_tensor(sc[:, :, :, :], sc[:, :, :, :], topv.unsqueeze(2).to_broadcast([P, QT * B, B, H]), ALU.mult))
        for j in range(QT):
            for s in range(B):
                settle()
                for t in range(s + 1):
                    pr = sc[:, B * j + s, t, :].rearrange("p (g r d) -> p g r d", g=EH, d=1).to_broadcast([P, EH, REP, DK])
                    step(nc.vector.tensor_tensor(prod[:, t, :].rearrange("p (g r d) -> p g r d", g=EH, r=REP),
                                                 pr, shared(QT * t + j, D + EH * DK), ALU.mult))
                settle()
                out = ao[:, QT * s + j, :]
                if s == 0:
                    last = nc.vector.tensor_copy(out, prod[:, 0, :])
                else:
                    last = nc.vector.tensor_reduce(out, prod[:, 0:s + 1, :].rearrange("p t c -> p c t"), axis=AX.X, op=ALU.add)
                step(last)
        settle()
        nc.vector.nop().then_inc(ao_set, 1)
        for s in range(B):
            dve.wait_ge(full_set, turn_full(4 + s))
            nc.vector.tensor_tensor(yT_lo[:, :, :], wide[s % 2][:, :, :], yT_hi[:, :, :].bitcast(F32), ALU.subtract).then_inc(parts_set, 1)
            for t in range(QT):
                i = QT * s + t
                dve.wait_ge(product_ready, NT + i + 1)
                nc.vector.tensor_tensor(h0[:, i, :], narrow[(NT + i) % 3][:, 0:D], h0[:, i, :], ALU.add).then_inc(added, 1)
        dve.wait_ge(added, NT)
        nc.vector.nop().then_inc(x2_set, 1)
        statistics(2, h0)
        normalise_turn(8)
        normalise_turn(9)
        for s in range(B):
            part = slice(512 * s, 512 * s + 512)
            split_turn(8 + s, y2_hi[:, :, part], y2_lo[:, :, part])
            if s + 2 < B:
                normalise_turn(8 + s + 2)

        def per_tile(a):
            return a.unsqueeze(2).to_broadcast([P, NT, E_])

        dve.wait_ge(logits_ready, 1)
        lv = values[:, 0:NT * E_].rearrange("p (t e) -> p t e", e=E_)
        step(nc.vector.tensor_reduce(lmax[:, :], lv, axis=AX.X, op=ALU.max))
        settle()
        nc.vector.tensor_tensor(logits[:, :, :], lv, per_tile(lmax[:, :]), ALU.subtract).then_inc(shifted, 1)
        dve.wait_ge(gate_exps, 1)
        step(nc.vector.tensor_reduce(gsum[:, :], logits[:, :, :], axis=AX.X, op=ALU.add))
        settle()
        step(nc.vector.reciprocal(lmax[:, :], gsum[:, :]))
        settle()
        step(nc.vector.tensor_tensor(logits[:, :, :], logits[:, :, :], per_tile(lmax[:, :]), ALU.mult))
        settle()
        for t in range(NT):
            step(nc.vector.max(best[:, t, :], logits[:, t, :]))
        settle()
        for t in range(NT):
            step(nc.vector.max_index(which[:, t, :], best[:, t, :], logits[:, t, :]))
        settle()
        numbers = iota[:, :].unsqueeze(1).to_broadcast([P, NT, E_])
        for i, dst in ((0, gates), (1, chosen)):
            step(nc.vector.tensor_tensor(dst[:, :, :], numbers, per_tile(which[:, :, i]), ALU.is_equal))
            settle()
            step(nc.vector.tensor_tensor(dst[:, :, :], dst[:, :, :], per_tile(best[:, :, i]), ALU.mult))
            settle()
        step(nc.vector.tensor_tensor(gates[:, :, :], gates[:, :, :], chosen[:, :, :], ALU.add))
        settle()

    @block.tensor
    def _(pe):
        pe.wait_ge(const_in, 48)

        def transposes(turn, src):
            if turn >= 2:
                pe.wait_ge(parts_set, turn - 1)
            for k in range(KC):
                for t in range(QT):
                    last = nc.tensor.transpose(wide[turn % 2][:, k, P * t:P * t + P], src(t)[:, P * k:P * k + P], ident[:, :])
            last.then_inc(transposed, 1)

        def products(out, hi, lo, t, w_hi, w_lo):
            for i, (a, c) in enumerate(((hi, w_hi), (hi, w_lo), (lo, w_hi))):
                for k in range(KC):
                    last = nc.tensor.matmul(out, a[:, k, P * t:P * t + P], c[:, k, :], start=(i, k) == (0, 0), stop=(i, k) == (2, KC - 1))
            return last

        def first_turn(s):
            pe.wait_ge(norm_set, s + 1)
            transposes(s, lambda t: norm[:, s % 2, t, :])

        first_turn(0)
        for s in range(B):
            if s + 1 < B:
                first_turn(s + 1)
            pe.wait_ge(parts_set, s + 1)
            pe.wait_ge(w_split, 1)
            for t in range(QT):
                i = QT * s + t
                if i >= 3:
                    pe.wait_ge(qkv_copied, i - 2)
                products(narrow[i % 3][:, 0:QKV], yT_hi, yT_lo, t, qkvw_hi, qkvw_lo).then_inc(product_ready, 1)
        pe.wait_ge(ao_set, 1)
        pe.wait_ge(w_split, 2)
        transposes(4, lambda t: ao[:, t, :])
        for s in range(B):
            if s + 1 < B:
                transposes(4 + s + 1, lambda t: ao[:, QT * (s + 1) + t, :])
            pe.wait_ge(parts_set, 4 + s + 1)
            for t in range(QT):
                i = QT * s + t
                if i >= 3:
                    pe.wait_ge(added, i - 2)
                products(narrow[(NT + i) % 3][:, 0:D], yT_hi, yT_lo, t, projw_hi, projw_lo).then_inc(product_ready, 1)

        def last_turn(s):
            pe.wait_ge(norm_set, 4 + s + 1)
            transposes(8 + s, lambda t: norm[:, s % 2, t, :])

        last_turn(0)
        pe.wait_ge(w_split, 3)
        for s in range(B):
            if s + 1 < B:
                last_turn(s + 1)
            pe.wait_ge(parts_set, 8 + s + 1)
            for t in range(QT):
                i = QT * s + t
                last = products(values[:, E_ * i:E_ * i + E_], y2_hi, y2_lo, i, rw_hi, rw_lo)
        last.then_inc(logits_ready, 1)


def experts(nc, ctx, io, xt, y2_hi, y2_lo, gates, W, wide, narrow, values, out):
    def sb(name, shape, dt):
        return ctx.enter_context(nc.sbuf_tensor(name, shape, dt))

    def sem(name):
        return ctx.enter_context(nc.semaphore(name))

    CH = 512
    NCH = NT * P // CH
    TC = CH // P
    chunks = E_ * NCH
    hid = [sb(f"hid{i}", [P, FC, CH], F32) for i in range(2)]
    hid_hi = [sb(f"hid_hi{i}", [P, FC, CH], F32R) for i in range(2)]
    hid_lo = [sb(f"hid_lo{i}", [P, FC, CH], F32R) for i in range(2)]
    up_banks = [wide[f // 2][:, f % 2, :] for f in range(FC)]
    down_banks = [narrow[0], narrow[1], narrow[2], values]
    up_ready, gelu_done, hi_set, parts_set = sem("up_ready"), sem("gelu_done"), sem("hid_hi_set"), sem("hid_parts_set")
    down_ready, summed, stored = sem("down_ready"), sem("summed"), sem("stored")

    block = ctx.enter_context(nc.Block())

    @block.sync
    def _(sp):
        for e in range(2, E_):
            load_expert(sp, nc, W, io, e)
        for c in range(NCH):
            sp.wait_ge(summed, TC * (chunks - NCH + c + 1))
            sp.dma_start(out[CH * c:CH * c + CH, :].rearrange("(t p) d -> p t d", p=P), xt[:, TC * c:TC * c + TC, :]).then_inc(stored, 16)
        sp.wait_ge(stored, 16 * NCH)

    @block.gpsimd
    def _(pool):
        for e in range(2, E_):
            pool.wait_ge(down_ready, TC * NCH * (e - 1))
            split_expert(pool, nc, W, e)

    @block.scalar
    def _(act):
        for m in range(chunks):
            for f in range(FC):
                act.wait_ge(up_ready, FC * m + f + 1)
                if m >= 2:
                    act.wait_ge(parts_set, FC * (m - 2) + f + 1)
                nc.scalar.activation(hid[m % 2][:, f, :], up_banks[f], ACT.Gelu_apprx_tanh).then_inc(gelu_done, 1)

    @block.vector
    def _(dve):
        def split(m):
            i = m % 2
            if m >= 2:
                dve.wait_ge(down_ready, TC * (m - 1))
            for f in range(FC):
                dve.wait_ge(gelu_done, FC * m + f + 1)
                nc.vector.tensor_copy(hid_hi[i][:, f, :], hid[i][:, f, :]).then_inc(hi_set, 1)
            for f in range(FC):
                dve.wait_ge(hi_set, FC * m + f + 1)
                nc.vector.tensor_tensor(hid_lo[i][:, f, :], hid[i][:, f, :], hid_hi[i][:, f, :].bitcast(F32), ALU.subtract).then_inc(parts_set, 1)

        split(0)
        for m in range(chunks):
            if m + 1 < chunks:
                split(m + 1)
            e, c = divmod(m, NCH)
            for j in range(TC):
                t = TC * c + j
                dve.wait_ge(down_ready, TC * m + j + 1)
                if e > 0:
                    dve.wait_ge(summed, TC * (m - NCH) + j + 1)
                nc.vector.scalar_tensor_tensor(out=xt[:, t, :], in0=down_banks[j][:, 0:D], scalar=gates[:, t, e:e + 1],
                                               in1=xt[:, t, :], op0=ALU.mult, op1=ALU.add).then_inc(summed, 1)

    @block.tensor
    def _(pe):
        def up(m):
            e, c = divmod(m, NCH)
            if c == 0:
                pe.wait_ge(W.split, e + 1)
            cols = slice(CH * c, CH * c + CH)
            for f in range(FC):
                rows = slice(P * f, P * f + P)
                if m >= 1:
                    pe.wait_ge(gelu_done, FC * (m - 1) + f + 1)
                for i, (w, y) in enumerate(((W.w1_hi, y2_hi), (W.w1_hi, y2_lo), (W.w1_lo, y2_hi))):
                    for k in range(KC):
                        last = nc.tensor.matmul(up_banks[f], w[e % 2][:, k, rows], y[:, k, cols], start=(i, k) == (0, 0), stop=(i, k) == (2, KC - 1))
                last.then_inc(up_ready, 1)

        def down(m):
            e, i = m // NCH, m % 2
            pe.wait_ge(parts_set, FC * (m + 1))
            for j in range(TC):
                toks = slice(P * j, P * j + P)
                if m >= 1:
                    pe.wait_ge(summed, TC * (m - 1) + j + 1)
                n = 0
                for h, w in ((hid_hi, W.w2_hi), (hid_hi, W.w2_lo), (hid_lo, W.w2_hi)):
                    for f in range(FC):
                        last = nc.tensor.matmul(down_banks[j][:, 0:D], h[i][:, f, toks], w[e % 2][:, f, :], start=n == 0, stop=n == 3 * FC - 1)
                        n += 1
                last.then_inc(down_ready, 1)

        up(0)
        for m in range(chunks):
            if m + 1 < chunks:
                up(m + 1)
            down(m)


def tables():
    inv = 1.0 / np.float32(10000.0) ** (np.arange(0, DK, 2, dtype=np.float32) / DK)
    ang = np.repeat(np.arange(SK, dtype=np.float32)[:, None] * inv.astype(np.float32)[None, :], 2, axis=-1)
    sign = np.where(np.arange(DK) % 2 == 0, -1.0, 1.0).astype(np.float32)
    c = np.cos(ang).reshape(KT, P, DK).transpose(1, 0, 2)
    s = (np.sin(ang) * sign).reshape(KT, P, DK).transpose(1, 0, 2)
    return {"cos": np.ascontiguousarray(c), "sin": np.ascontiguousarray(s), "ident": np.eye(P, dtype=np.float32),
            "iota": np.tile(np.arange(E_, dtype=np.float32), (P, 1)),
            "mask_coef": np.tile(np.array(MASK_PARTS, np.float32), B)[:, None]}


def program(nc, io, out):
    with ExitStack() as ctx:
        xt = ctx.enter_context(nc.sbuf_tensor("xt", [P, NT, D], F32))
        wide = [ctx.enter_context(nc.psum_tensor(f"wide{i}", [P, 2, 512], F32)) for i in range(2)]
        narrow = [ctx.enter_context(nc.psum_tensor(f"narrow{i}", [P, 512], F32)) for i in range(3)]
        values = ctx.enter_context(nc.psum_tensor("values", [P, 512], F32))
        with ExitStack() as part:
            cross_attention(nc, part, io, xt, wide, narrow, values)
        y2_hi = ctx.enter_context(nc.sbuf_tensor("y2_hi", [P, KC, NT * P], F32R))
        y2_lo = ctx.enter_context(nc.sbuf_tensor("y2_lo", [P, KC, NT * P], F32R))
        gates = ctx.enter_context(nc.sbuf_tensor("gates", [P, NT, E_], F32))
        W = expert_weights(nc, ctx, io)
        with ExitStack() as part:
            attention_and_router(nc, part, io, xt, y2_hi, y2_lo, gates, W, wide, narrow, values)
        with ExitStack() as part:
            experts(nc, part, io, xt, y2_hi, y2_lo, gates, W, wide, narrow, values, out)


def kernel(**inputs):
    import concourse.bacc as _bacc
    from concourse.bass_utils import run_bass_kernel_spmd as _run

    a = {k: np.asarray(v) for k, v in inputs.items()}
    T = np.ascontiguousarray
    arrays = {
        "x": T(a["x"].reshape(B * SQ, D)),
        "ctxT": T(a["ctx_1024"].reshape(B * SK, D).T),
        "mask_col": T(a["mask_BxS2_ik0"].reshape(B * KT, P).T),
        "mask_row": T(np.repeat(a["mask_BxS2_ik0"], 2, axis=0)),
        **{"w" + w: T(a["L0_xattn_w_" + w].T) for w in "qkvo"},
        "wqkv": T(a["L0_ffn_qkv_weight"].T),
        "wproj": T(a["L0_ffn_proj_weight"].T),
        "router": T(a["L0_ffn_router_weight"].T),
        "w1": T(a["L0_ffn_moe_w1"]),
        "w2": T(a["L0_ffn_moe_w2"]),
        "lncol": T(np.stack([a["L0_ffn_ln1_weight"], a["L0_ffn_ln1_bias"], a["L0_ffn_ln2_weight"],
                             a["L0_ffn_ln2_bias"]]).reshape(4, KC, P).transpose(2, 0, 1)),
        **tables(),
    }
    nc = _bacc.Bacc("TRN2", target_bir_lowering=False, num_devices=1)
    io = {n: nc.dram_tensor("in_" + n, v.shape, mybir.dt.from_np(v.dtype), kind="ExternalInput").ap() for n, v in arrays.items()}
    out = nc.dram_tensor("out", (B * SQ, D), F32, kind="ExternalOutput").ap()
    program(nc, io, out)
    r = _run(nc, [{"in_" + n: v for n, v in arrays.items()}], core_ids=[0])
    return r.results[0]["out"].reshape(B, SQ, D)
```

```python
import numpy as np
import concourse.bass as bass
from concourse import mybir
from contextlib import ExitStack

F32 = mybir.dt.float32
F32R = mybir.dt.float32r
BF16 = mybir.dt.bfloat16
I32 = mybir.dt.int32
ALU = mybir.AluOpType
ACT = mybir.ActivationFunctionType
AX = mybir.AxisListType

P = 128
B, SQ, SK, D = 4, 512, 1024, 256
H, DK = 16, 16
KC = D // P
QT, KT = SQ // P, SK // P
NT = B * QT
EPS = 1e-5
MASKED = -10000.0
HH = H // 2
UNITS = 2 * B
CD = D // HH
QUADS = 2 * UNITS
GROUPS = QUADS * KT
PIECE_RUNS = ((0, 3), (1, 2), (2, 1))
R_MASK = sum(n for _, n in PIECE_RUNS) * DK
R_MAX = R_MASK + 2
R_ALL = R_MAX + 3
MASK_PARTS = (-39936.0, -64.0)
assert sum(MASK_PARTS) == MASKED * DK ** 0.5


def attention_jobs():
    def proj(b):
        jobs = [("xT", b)] + [("q", b, j) for j in range(QT)] + [("trq", b)]
        for g in range(2):
            jobs += [("kv", b, g * 4 + j) for j in range(4)] + [("trk", b, g)]
        return jobs

    def maxes(quad):
        return [("max", quad, h, qt) for h in range(4) for qt in range(QT)] + [("mxt", quad)]

    def interleave(many, few):
        out, n = [], 0
        for i, j in enumerate(many):
            out.append(j)
            while n < len(few) and (n + 1) * len(many) <= (i + 1) * len(few):
                out.append(few[n])
                n += 1
        return out + few[n:]

    cost = {"xT": 1.5, "q": .85, "kv": 1.4, "trq": 2., "trk": 2., "max": 1.13, "mxt": 2.}
    before = proj(0) + proj(1)[:EARLY] + maxes(0)
    places = [[] for _ in range(GROUPS)]
    for b in range(B):
        work = sum((maxes(4 * b + i) for i in range(1, 5 if b + 1 < B else 4)), [])
        if b == 0:
            work = work[:17] + interleave(work[17:34], proj(1)[EARLY:]) + work[34:]
        elif b + 1 < B:
            work = work[:23] + interleave(work[23:40], proj(b + 1)[1:]) + work[40:]
        first = max(32 * b - LEAD, 0)
        last = 32 * b + 32 - LEAD if b + 1 < B else GROUPS - 8 - LEAD
        total, spent = sum(cost[j[0]] for j in work), 0.0
        for j in work:
            places[first + int(spent / total * (last - first))].append(j)
            spent += cost[j[0]]
    for quad in range(QUADS - 1):
        places[8 * quad + 9].insert(1, ("out", quad))
    for b in range(B - 1):
        if b > 0:
            places[32 * b + 4].insert(1, ("xT", b + 1))
        places[32 * b + 34].insert(1, ("oT", b))
        places[32 * b + 35].insert(1, ("oP", b))
    after = [("out", QUADS - 1), ("oT", B - 1), ("oP", B - 1)]
    jobs = before + [j for now in places for j in now] + after
    index = {j: n for n, j in enumerate(jobs)}
    for b in range(B - 1):
        assert index[("oT", b)] < index[("oP", b)] < index.get(("xT", b + 2), len(jobs))
        assert index.get(("oP", b - 1), -1) < index[("xT", b + 1)] < index[("q", b + 1, 0)]
        assert index[("xT", b + 1)] < index[("out", 4 * b)]
    return index, before, places, after


EARLY = 11
LEAD = 4


def cross_attention(nc, ctx, io, xt, wide, narrow, values):
    index, before, places, after = attention_jobs()
    jobs = sorted(index, key=index.get)

    def sb(name, shape, dt):
        return ctx.enter_context(nc.sbuf_tensor(name, shape, dt))

    def sem(name):
        return ctx.enter_context(nc.semaphore(name))

    ident = sb("ident", [P, P], F32)
    w_hi = {w: sb(f"w{w}_hi", [P, KC, D], F32R) for w in "qkvo"}
    w_lo = {w: sb(f"w{w}_lo", [P, KC, D], F32R) for w in "qkvo"}
    cos = sb("cos", [P, KT, CD], F32)
    sin = sb("sin", [P, KT, CD], F32)
    mcol_i = sb("mcol_i", [P, B * KT], I32)
    mcol = sb("mcol", [P, B * KT], F32)
    kcos = sb("kcos", [P, 2, KT, CD], F32)
    ksin = sb("ksin", [P, 2, KT, CD], F32)
    mcoef = sb("mcoef", [2 * B, 1], F32)
    mrow = sb("mrow", [2 * B, SK], BF16)
    stats = sb("stats", [P, NT, 6], F32)
    mv = sb("mv", [P, NT, 2], F32)
    varc = sb("varc", [P, NT], F32)
    std = sb("std", [P, NT], F32)
    rstd = sb("rstd", [P, NT], F32)
    xT_hi = sb("xT_hi", [P, KC, SQ], F32R)
    xT_lo = sb("xT_lo", [P, KC, SQ], F32R)
    craw = sb("craw", [P, KC, 512], F32)
    c_hi = sb("c_hi", [P, KC, SK], F32R)
    c_lo = sb("c_lo", [P, KC, SK], F32R)
    rope_b = sb("rope_b", [P, 2, D], F32)
    roped = sb("roped", [P, 8, D], F32)
    pieces = sb("pieces", [P, 2, 3, KC, 512], BF16)
    rest = sb("rest", [P, KC, 512], F32)
    qst = [sb(f"qst{i}", [R_ALL, HH, SQ], BF16) for i in range(3)]
    kst = [sb(f"kst{i}", [R_ALL, HH, SK], BF16) for i in range(3)]
    mx = [sb(f"mx{i}", [P, QT * 4], F32) for i in range(2)]
    mxp = sb("mxp", [4, 3, SQ], BF16)
    vaug = [sb(f"vaug{i}", [P, KT, H, DK + 1], F32) for i in range(2)]
    NP = 7
    probs = sb("probs", [P, NP, SQ], F32)
    wraw = {w: probs[:, n, :].rearrange("p (k d) -> p k d", k=KC) for n, w in enumerate("qkvo")}
    mrow_i = probs[0:2 * B, 4:6, :].rearrange("r a n -> r (a n)").bitcast(I32)
    ones = probs[0:8, 6, 0:256].bitcast(BF16)
    outT = sb("outT", [P, SQ], F32)
    rec = sb("rec", [P, 16], F32)
    attn = sb("attn", [P, QT, D], F32)
    xn = attn
    aT_hi, aT_lo = xT_hi, xT_lo
    q_dram = nc.dram_tensor("q_pieces", [B, 3, KC, P, SQ], BF16, kind="Internal").ap()
    m_dram = nc.dram_tensor("m_pieces", [QUADS, 4, 3, SQ], BF16, kind="Internal").ap()
    k_dram = nc.dram_tensor("k_pieces", [B, 3, KC, P, SK], BF16, kind="Internal").ap()

    x_in = [sem(f"x_in{b}") for b in range(B)]
    w_in, tab_in, c_in = sem("w_in"), sem("tab_in"), sem("c_in")
    ones_set, ones_in = sem("ones_set"), sem("ones_in")
    stack_in = [sem(f"stack_in{i}") for i in range(3)]
    maxrow_in, maxrow_out = [sem(f"maxrow_in{i}") for i in range(2)], sem("maxrow_out")
    pieces_out = [sem(f"pieces_out{i}") for i in range(2)]
    w_split, c_high, c_split, mask_set = sem("w_split"), sem("c_high"), sem("c_split"), sem("mask_set")
    var_set, std_set, xn_set, values_prepared = sem("var_set"), sem("std_set"), sem("xn_set"), sem("values_prepared")
    dve_step = sem("dve_step")
    pe_done, dve_done, act_done, pool_done = sem("pe_done"), sem("dve_done"), sem("act_done"), sem("pool_done")
    score_ready, exp_done, pv_done, outT_set = sem("score_ready"), sem("exp_done"), sem("pv_done"), sem("outT_set")

    STACK = 16 * (2 * len(PIECE_RUNS) + 1)
    SPLIT = ("xT", "trq", "trk", "mxt", "oT")
    ACT_KINDS = SPLIT + ("kv",)
    POOL_KINDS = ("q", "kv", "trq", "trk")
    PIECED = ("trq", "trk")

    def act_count(n):
        return sum(j[0] in ACT_KINDS for j in jobs[:n + 1])

    def pool_count(n):
        return sum(j[0] in POOL_KINDS for j in jobs[:n + 1])

    def last_before(n, kinds):
        return max((m for m in range(n) if jobs[m][0] in kinds), default=-1)

    high_context = {("kv", 0, 0): 1, ("trk", 0, 0): 2, ("trk", 0, 1): 3, ("mxt", 1): 4, ("mxt", 2): 5, ("trk", 2, 1): 6, ("mxt", 8): 7}
    assert sorted(high_context, key=index.get) == list(high_context) and len(high_context) == 2 * B - 1
    assert all(index[j] < index[("kv", i // 2, 4 * (i % 2))] for j, i in high_context.items())

    def tile_number(j):
        return j[1] * (QT + KT) + (j[2] if j[0] == "q" else QT + j[2])

    def transposed_by(tile):
        b, r = divmod(tile, QT + KT)
        return index[("trq", b) if r < QT else ("trk", b, (r - QT) // 4)]

    def piece_job(j):
        return 3 * j[1] + (0 if j[0] == "trq" else 1 + j[2])

    def pieces_stored(last, i):
        return sum(t % 2 == i for t in range(last + 1))

    block = ctx.enter_context(nc.Block())

    @block.sync
    def _(sp):
        def load_x(b):
            sp.dma_start(xt[:, QT * b:QT * b + QT, :],
                         io["x"][SQ * b:SQ * b + SQ, :].rearrange("(t p) d -> p t d", p=P)).then_inc(x_in[b], 16)

        def load_context(i):
            if i > 0:
                sp.wait_ge(c_split, i)
            sp.dma_start(craw[:, :, :], io["ctxT"][:, 512 * i:512 * i + 512].rearrange("(k p) t -> p k t", p=P)).then_inc(c_in, 16)

        def load_stack(u):
            b, c = divmod(u, 2)
            if u >= 3:
                sp.wait_ge(score_ready, 64 * (u - 2))
            row = 0
            for piece, n in PIECE_RUNS:
                rows = slice(row, row + DK * n)
                sp.dma_start(qst[u % 3][rows, :, :].rearrange("r h t -> r (h t)"),
                             q_dram[b, piece, c].rearrange("(d h) t -> d (h t)", h=HH)
                             .unsqueeze(0).to_broadcast([n, DK, HH * SQ])).then_inc(stack_in[u % 3], 16)
                sp.dma_start(kst[u % 3][rows, :, :].rearrange("r h t -> r (h t)"),
                             k_dram[b, 0:n, c].rearrange("a (d h) t -> a d (h t)", h=HH)).then_inc(stack_in[u % 3], 16)
                row += DK * n
            sp.dma_start(kst[u % 3][R_MASK:R_MAX, :, :],
                         mrow[2 * b:2 * b + 2, :].unsqueeze(1).to_broadcast([2, HH, SK])).then_inc(stack_in[u % 3], 16)

        def load_max_rows(quad):
            u, h = quad // 2, 4 * (quad % 2)
            sp.wait_ge(dve_done, index[("mxt", quad)] + 1)
            sp.dma_start(m_dram[quad], mxp[:, :, :]).then_inc(maxrow_out, 16)
            sp.wait_ge(maxrow_out, 16 * (quad + 1))
            if quad >= 2:
                sp.wait_ge(score_ready, 32 * (quad - 2) + 1)
            sp.dma_start(qst[u % 3][R_MAX:R_ALL, h:h + 4, :], m_dram[quad].rearrange("h a t -> a h t")).then_inc(maxrow_in[quad % 2], 16)

        def store_pieces(j):
            sp.wait_ge(pool_done, pool_count(index[j]))
            dst = q_dram[j[1]] if j[0] == "trq" else k_dram[j[1]][:, :, :, 512 * j[2]:512 * j[2] + 512]
            sp.dma_start(dst.rearrange("a c p t -> p (a c) t"),
                         pieces[:, piece_job(j) % 2, :, :, :].rearrange("p a c t -> p (a c) t")).then_inc(pieces_out[piece_job(j) % 2], 16)

        def batch_stored(b):
            for i in range(2):
                sp.wait_ge(pieces_out[i], 16 * pieces_stored(3 * b + 2, i))

        load_x(0)
        load_context(0)
        for dst, name in ((ident[:, :], "ident"), (mcol_i[:, :], "mask_col"), (mrow_i, "mask_row"), (mcoef[:, :], "mask_coef")):
            sp.dma_start(dst, io[name]).then_inc(tab_in, 16)
        sp.dma_start(cos[:, :, :], io["cos"]).then_inc(tab_in, 16)
        sp.dma_start(sin[:, :, :], io["sin"]).then_inc(tab_in, 16)
        for b in range(1, B):
            load_x(b)
        load_context(1)
        load_context(2)
        sp.wait_ge(ones_in, 6 * 16)
        sp.wait_ge(mask_set, 1)
        store_pieces(("trq", 0))
        store_pieces(("trk", 0, 0))
        load_context(3)
        store_pieces(("trk", 0, 1))
        batch_stored(0)
        load_stack(0)
        load_stack(1)
        store_pieces(("trq", 1))
        store_pieces(("trk", 1, 0))
        load_context(4)
        load_max_rows(0)
        for b in range(B):
            load_max_rows(4 * b + 1)
            if b == 0:
                load_context(5)
            load_max_rows(4 * b + 2)
            if b == 0:
                store_pieces(("trk", 1, 1))
                load_context(6)
                batch_stored(1)
                load_stack(2)
            elif b + 1 < B:
                store_pieces(("trq", b + 1))
                store_pieces(("trk", b + 1, 0))
                store_pieces(("trk", b + 1, 1))
                batch_stored(b + 1)
                load_stack(2 * b + 2)
                if b == 1:
                    load_context(7)
            load_max_rows(4 * b + 3)
            if b + 1 < B:
                load_stack(2 * b + 3)
                load_max_rows(4 * b + 4)

    @block.gpsimd
    def _(pool):
        nc.gpsimd.memset(ones[:, :], 1.0).then_inc(ones_set, 1)

        for i in range(3):
            for st, n in ((qst[i], HH), (kst[i], 2 * HH)):
                pool.wait_ge(ones_set, 1)
                pool.dma_start(st[R_MASK:R_ALL, :, :].rearrange("r h (a n) -> r (h a) n", n=512),
                               ones[0:R_ALL - R_MASK, :].unsqueeze(1).to_broadcast([R_ALL - R_MASK, n, 512])).then_inc(ones_in, 16)

        def split_context(i):
            part = slice(512 * (i % 2), 512 * (i % 2) + 512)
            pool.wait_ge(c_high, i + 1)
            nc.gpsimd.tensor_tensor(c_lo[:, :, part], craw[:, :, :], c_hi[:, :, part].bitcast(F32), ALU.subtract).then_inc(c_split, 1)

        for i in range(2):
            nc.gpsimd.memset(vaug[i][:, :, :, DK:DK + 1], 1.0).then_inc(values_prepared, 1)
        split_context(0)

        def job(j):
            n, kind = index[j], j[0]
            if kind not in POOL_KINDS:
                if j in high_context:
                    split_context(high_context[j])
                return
            pool.wait_ge(dve_done, n + 1)
            if kind in ("q", "kv"):
                r = tile_number(j)
                nc.gpsimd.tensor_tensor(roped[:, r % 8, :], roped[:, r % 8, :], rope_b[:, r % 2, :], ALU.add).then_inc(pool_done, 1)
            else:
                i = piece_job(j) % 2
                nc.gpsimd.tensor_tensor(pieces[:, i, 2, :, :], rest[:, :, :], pieces[:, i, 1, :, :], ALU.subtract).then_inc(pool_done, 1)
            if j in high_context:
                split_context(high_context[j])

        for j in jobs:
            job(j)

    @block.scalar
    def _(act):
        for w in "qkvo":
            act.dma_start(wraw[w], io["w" + w].rearrange("(k p) n -> p k n", p=P)).then_inc(w_in, 16)
        def deviation(i, tiles):
            act.wait_ge(var_set, i + 1)
            nc.scalar.activation(std[:, tiles], varc[:, tiles], ACT.Sqrt).then_inc(std_set, 1)

        deviation(0, slice(0, QT))

        def job(j):
            n, kind = index[j], j[0]
            if kind not in ACT_KINDS:
                return
            act.wait_ge(pe_done, n + 1)
            src = wide[n % 2]
            if kind == "kv":
                b, kt = j[1:]
                if kt == 0:
                    if b < 2:
                        act.wait_ge(values_prepared, 3)
                    else:
                        act.wait_ge(pv_done, 32 * (b - 1))
                nc.scalar.activation(vaug[b % 2][:, kt, :, 0:DK],
                                     src[:, 1, 0:D].rearrange("p (h d) -> p h d", h=H), ACT.Copy).then_inc(act_done, 1)
                return
            if kind in ("xT", "oT"):
                m = last_before(n, ("q", "oP"))
                if m >= 0:
                    act.wait_ge(pe_done, m + 1)
                dst, src = xT_hi[:, :, :], src[:, :, :]
            elif kind in ("trq", "trk"):
                if piece_job(j) >= 2:
                    act.wait_ge(pieces_out[piece_job(j) % 2], 16 * (piece_job(j) // 2))
                dst, src = pieces[:, piece_job(j) % 2, 0, :, :], src[:, :, :]
            else:
                if j[1] > 0:
                    act.wait_ge(maxrow_out, 16 * j[1])
                dst, src = mxp[:, 0, :], src[0:4, 0, :]
            nc.scalar.activation(dst, src, ACT.Copy).then_inc(act_done, 1)

        def exponential(g, hq):
            n = 4 * g + hq
            act.wait_ge(score_ready, n + 1)
            if n >= NP:
                act.wait_ge(pv_done, (n - NP) // 4 + 1)
            nc.scalar.activation(probs[:, n % NP, :], narrow[n % 3][:, :], ACT.Exp, scale=DK ** -0.5).then_inc(exp_done, 1)

        def take_out(quad):
            act.wait_ge(pv_done, 8 * (quad + 1))
            if quad >= 1:
                act.wait_ge(pe_done, index[("out", quad - 1)] + 1)
            nc.scalar.activation(outT[:, :], values[:, :], ACT.Copy).then_inc(outT_set, 1)

        for j in before:
            job(j)
            if j == ("kv", 0, 4):
                deviation(1, slice(QT, NT))
        for g in range(GROUPS):
            now = places[g]
            exponential(g, 0)
            exponential(g, 1)
            for j in now[0:1]:
                job(j)
            exponential(g, 2)
            if g % 8 == 0 and g > 0:
                take_out(g // 8 - 1)
            for j in now[1:2]:
                job(j)
            exponential(g, 3)
            for j in now[2:]:
                job(j)
        take_out(QUADS - 1)
        for j in after:
            job(j)

    @block.vector
    def _(dve):
        steps = [0]

        def step(ins):
            steps[0] += 1
            ins.then_inc(dve_step, 1)

        def settle():
            dve.wait_ge(dve_step, steps[0])

        nc.vector.memset(values[:, :], 0.0).then_inc(values_prepared, 1)
        def statistics(batches):
            for b in batches:
                dve.wait_ge(x_in[b], 16)
                for t in range(QT * b, QT * b + QT):
                    step(nc.vector.bn_stats(stats[:, t, :], xt[:, t, :]))
            settle()
            tiles = slice(QT * batches[0], QT * batches[-1] + QT)
            for t in range(tiles.start, tiles.stop):
                step(nc.vector.bn_aggr(mv[:, t, :], stats[:, t, :]))
            settle()
            nc.vector.tensor_scalar_add(varc[:, tiles], mv[:, tiles, 1], EPS).then_inc(var_set, 1)

        def deviations(i, tiles):
            dve.wait_ge(std_set, i + 1)
            step(nc.vector.reciprocal(rstd[:, tiles], std[:, tiles]))
            settle()

        def split_weight(w):
            step(nc.vector.tensor_copy(w_hi[w][:, :, :], wraw[w]))
            settle()
            nc.vector.tensor_tensor(w_lo[w][:, :, :], wraw[w], w_hi[w][:, :, :].bitcast(F32), ALU.subtract).then_inc(w_split, 1)

        def key_tables(b):
            for out, table in ((kcos, cos), (ksin, sin)):
                step(nc.vector.tensor_tensor(out[:, b % 2, :, :], table[:, :, :],
                                             mcol[:, KT * b:KT * b + KT].unsqueeze(2).to_broadcast([P, KT, CD]), ALU.mult))

        def normalise(b):
            for t in range(QT):
                nc.vector.tensor_scalar(xn[:, t, :], xt[:, QT * b + t, :], mv[:, QT * b + t, 0:1],
                                        rstd[:, QT * b + t:QT * b + t + 1], ALU.subtract, ALU.mult).then_inc(xn_set, 1)

        def high_part(i):
            b, g = divmod(i, 2)
            dve.wait_ge(c_in, 16 * (i + 1))
            if b > 0:
                dve.wait_ge(pe_done, index[("kv", b - 1, 4 * g + 3)] + 1)
            nc.vector.tensor_copy(c_hi[:, :, 512 * g:512 * g + 512], craw[:, :, :]).then_inc(c_high, 1)

        def masks():
            dve.wait_ge(tab_in, 96)
            step(nc.vector.tensor_scalar(mcol[:, :], mcol_i[:, :], 0.0, None, ALU.not_equal))
            nc.vector.tensor_scalar(mrow[:, :], mrow_i, 0.0, mcoef[:, 0:1], ALU.is_equal, ALU.mult).then_inc(mask_set, 1)
            settle()
            key_tables(0)

        statistics([0])
        dve.wait_ge(w_in, 64)
        split_weight("q")
        deviations(0, slice(0, QT))
        normalise(0)
        high_part(0)

        def job(j):
            n, kind = index[j], j[0]
            slot = wide[n % 2]
            dve.wait_ge(pe_done, n + 1)
            if kind in SPLIT:
                dve.wait_ge(act_done, act_count(n))
            if kind in PIECED or kind == "mxt":
                m = last_before(n, PIECED)
                if m >= 0:
                    dve.wait_ge(pool_done, pool_count(m))
                m = last_before(n, ("mxt",))
                if m >= 0:
                    dve.wait_ge(dve_done, m + 1)
            if kind in ("xT", "oT"):
                nc.vector.tensor_tensor(xT_lo[:, :, :], slot[:, :, :], xT_hi[:, :, :].bitcast(F32), ALU.subtract).then_inc(dve_done, 1)
                if kind == "xT" and 0 < j[1] < B - 1:
                    key_tables(j[1] + 1)
                if kind == "oT" and j[1] + 2 < B:
                    normalise(j[1] + 2)
            elif kind in ("q", "kv"):
                r = tile_number(j)
                if r >= 2:
                    before_last = [m for m in range(n) if jobs[m][0] in ("q", "kv")][-2]
                    dve.wait_ge(pool_done, pool_count(before_last))
                    if r >= 8:
                        dve.wait_ge(pe_done, transposed_by(r - 8) + 1)
                if kind == "q":
                    c, s = cos[:, j[2], :], sin[:, j[2], :]
                else:
                    c, s = kcos[:, j[1] % 2, j[2], :], ksin[:, j[1] % 2, j[2], :]
                    if j[2] == 0:
                        settle()
                a = roped[:, r % 8, :].rearrange("p (d h) -> p d h", h=HH)
                rot = rope_b[:, r % 2, :].rearrange("p (i two h) -> p i two h", two=2, h=HH)
                swapped = slot[:, 0, 0:D].rearrange("p (i two h) -> p i two h", two=2, h=HH)[:, :, ::-1, :]
                nc.vector.tensor_tensor(a, slot[:, 0, 0:D].rearrange("p (d h) -> p d h", h=HH),
                                        c.unsqueeze(2).to_broadcast([P, CD, HH]), ALU.mult)
                nc.vector.tensor_tensor(rot, swapped, s.rearrange("p (i two) -> p i two", two=2)
                                        .unsqueeze(3).to_broadcast([P, CD // 2, 2, HH]), ALU.mult).then_inc(dve_done, 1)
            elif kind in ("trq", "trk"):
                part = pieces[:, piece_job(j) % 2, :, :, :]
                step(nc.vector.tensor_tensor(rest[:, :, :], slot[:, :, :], part[:, 0, :, :], ALU.subtract))
                settle()
                nc.vector.tensor_copy(part[:, 1, :, :], rest[:, :, :]).then_inc(dve_done, 1)
            elif kind == "mxt":
                left = rest[0:4, 0, :]
                step(nc.vector.tensor_tensor(left, slot[0:4, 0, :], mxp[:, 0, :], ALU.subtract))
                settle()
                step(nc.vector.tensor_copy(mxp[:, 1, :], left))
                settle()
                nc.vector.tensor_tensor(mxp[:, 2, :], left, mxp[:, 1, :], ALU.subtract).then_inc(dve_done, 1)
            elif kind == "max":
                quad, h, qt = j[1:]
                if quad >= 2 and h == 0 and qt == 0:
                    dve.wait_ge(pe_done, index[("mxt", quad - 2)] + 1)
                nc.vector.tensor_reduce(mx[quad % 2][:, 4 * qt + h:4 * qt + h + 1], slot[:, :, :], axis=AX.XY, op=ALU.max,
                                        negate=True).then_inc(dve_done, 1)
            elif kind == "out":
                b, first = j[1] // 4, 64 * (j[1] % 4)
                if b > 0 and first == 0:
                    dve.wait_ge(pe_done, index[("oT", b - 1)] + 1)
                if j[1] > 0:
                    dve.wait_ge(dve_done, index[("out", j[1] - 1)] + 1)
                o = slot[:, 0, :].rearrange("p (q h e) -> p q h e", q=QT, e=32)
                step(nc.vector.reciprocal(rec[:, :].rearrange("p (q h e) -> p q h e", q=QT, e=1), o[:, :, :, DK:DK + 1]))
                settle()
                nc.vector.tensor_tensor(attn[:, :, first:first + 64].rearrange("p q (h d) -> p q h d", d=DK), o[:, :, :, 0:DK],
                                        rec[:, :].rearrange("p (q h e) -> p q h e", q=QT, e=1).to_broadcast([P, QT, 4, DK]),
                                        ALU.mult).then_inc(dve_done, 1)
            elif kind == "oP":
                b = j[1]
                xb = xt[:, QT * b:QT * b + QT, :]
                nc.vector.tensor_tensor(xb, slot[:, :, :].rearrange("p k (t d) -> p (k t) d", d=D), xb, ALU.add).then_inc(dve_done, 1)

        for j in jobs:
            job(j)
            if j == ("xT", 0):
                split_weight("k")
            elif j == ("q", 0, 1):
                split_weight("v")
            elif j == ("q", 0, 3):
                masks()
            elif j == ("kv", 0, 2):
                statistics(list(range(1, B)))
            elif j == ("kv", 0, 5):
                deviations(1, slice(QT, NT))
                normalise(1)
                key_tables(1)
            elif j == ("kv", 1, 1):
                split_weight("o")
            if j in high_context:
                high_part(high_context[j])

    @block.tensor
    def _(pe):
        pe.wait_ge(tab_in, 96)

        def project(out, hi, lo, t, w, cols=slice(0, D)):
            for i, (a, c) in enumerate(((hi, w_hi[w]), (hi, w_lo[w]), (lo, w_hi[w]))):
                for k in range(KC):
                    last = nc.tensor.matmul(out, a[:, k, P * t:P * t + P], c[:, k, cols],
                                            start=(i, k) == (0, 0), stop=(i, k) == (2, KC - 1))
            return last

        def job(j):
            n, kind = index[j], j[0]
            slot = wide[n % 2]
            if n >= 2:
                pe.wait_ge(dve_done, n - 1)
                if jobs[n - 2][0] == "kv":
                    pe.wait_ge(act_done, act_count(n - 2))
            if kind == "xT":
                pe.wait_ge(xn_set, QT * (j[1] + 1))
                for k in range(KC):
                    for t in range(QT):
                        last = nc.tensor.transpose(slot[:, k, P * t:P * t + P], xn[:, t, P * k:P * k + P], ident[:, :])
            elif kind == "q":
                if j[2] == 0:
                    m = index[("xT", j[1])]
                    pe.wait_ge(dve_done, m + 1)
                    pe.wait_ge(w_split, 1)
                last = project(slot[:, 0, 0:D], xT_hi, xT_lo, j[2], "q")
            elif kind == "kv":
                if j[2] == 0:
                    pe.wait_ge(c_split, j[1] + 1)
                    pe.wait_ge(w_split, 3)
                project(slot[:, 0, 0:D], c_hi, c_lo, j[2], "k")
                last = project(slot[:, 1, 0:D], c_hi, c_lo, j[2], "v")
            elif kind in ("trq", "trk"):
                b = j[1]
                first = (QT + KT) * b + (0 if kind == "trq" else QT + 4 * j[2])
                pe.wait_ge(pool_done, pool_count(last_before(n, ("q", "kv"))))
                for k in range(KC):
                    for t in range(4):
                        last = nc.tensor.transpose(slot[:, k, P * t:P * t + P], roped[:, (first + t) % 8, P * k:P * k + P], ident[:, :])
            elif kind == "max":
                quad, h, qt = j[1:]
                u, h = quad // 2, 4 * (quad % 2) + h
                if h == 0 and qt == 0:
                    pe.wait_ge(stack_in[u % 3], STACK * (u // 3 + 1))
                for k in range(2):
                    last = nc.tensor.matmul(slot[:, k, :], qst[u % 3][0:R_MAX, h, P * qt:P * qt + P],
                                            kst[u % 3][0:R_MAX, h, 512 * k:512 * k + 512], start=True, stop=True)
            elif kind == "mxt":
                pe.wait_ge(dve_done, n)
                for qt in range(QT):
                    last = nc.tensor.transpose(slot[0:4, 0, P * qt:P * qt + P], mx[j[1] % 2][:, 4 * qt:4 * qt + 4], ident[:, :])
            elif kind == "out":
                pe.wait_ge(outT_set, j[1] + 1)
                for qt in range(QT):
                    last = nc.tensor.transpose(slot[:, 0, P * qt:P * qt + P], outT[:, P * qt:P * qt + P], ident[:, :])
            elif kind == "oT":
                pe.wait_ge(dve_done, index[("out", 4 * j[1] + 3)] + 1)
                for k in range(KC):
                    for t in range(QT):
                        last = nc.tensor.transpose(slot[:, k, P * t:P * t + P], attn[:, t, P * k:P * k + P], ident[:, :])
            elif kind == "oP":
                pe.wait_ge(dve_done, index[("oT", j[1])] + 1)
                pe.wait_ge(w_split, 4)
                for t in range(QT):
                    last = project(slot[:, t // 2, D * (t % 2):D * (t % 2) + D], aT_hi, aT_lo, t, "o")
            last.then_inc(pe_done, 1)

        def score(g, hq):
            u, quad, kt = g // 16, g // 8, g % 8
            n, h = 4 * g + hq, 4 * (quad % 2) + hq
            if kt == 0 and hq == 0:
                pe.wait_ge(maxrow_in[quad % 2], 16 * (quad // 2 + 1))
            if n >= 3:
                pe.wait_ge(exp_done, n - 2)
            nc.tensor.matmul(narrow[n % 3][:, :], kst[u % 3][0:R_ALL, h, P * kt:P * kt + P],
                             qst[u % 3][0:R_ALL, h, :], start=True, stop=True).then_inc(score_ready, 1)

        def weigh(g):
            b, kt = g // 32, g % 8
            pe.wait_ge(exp_done, 4 * g + 4)
            if g == 0:
                pe.wait_ge(values_prepared, 3)
            if g % 32 == 0:
                pe.wait_ge(act_done, act_count(index[("kv", b, KT - 1)]))
            if kt == 0 and g > 0:
                pe.wait_ge(outT_set, g // 8)
            for hq in range(4):
                h = 4 * (g // 8 % 4) + hq
                last = nc.tensor.matmul(values[32 * hq:32 * hq + DK + 1, :], vaug[b % 2][:, kt, h, :], probs[:, (4 * g + hq) % NP, :],
                                        start=kt == 0, stop=kt == KT - 1)
            last.then_inc(pv_done, 1)

        for j in before:
            job(j)
        for g in range(GROUPS):
            now = places[g]
            score(g, 0)
            score(g, 1)
            for j in now[0:1]:
                job(j)
            score(g, 2)
            if g >= 1:
                weigh(g - 1)
            for j in now[1:2]:
                job(j)
            score(g, 3)
            for j in now[2:]:
                job(j)
        weigh(GROUPS - 1)
        for j in after:
            job(j)


E_, F, EH = 8, 512, 4
FC = F // P
REP = H // EH
QKV = D + 2 * EH * DK
LEAST = -3.4028234663852886e38


def expert_weights(nc, ctx, io):
    def sb(name, shape, dt):
        return ctx.enter_context(nc.sbuf_tensor(name, shape, dt))

    class Weights:
        raw1, raw2 = sb("raw1", [P, KC, F], F32), sb("raw2", [P, FC, D], F32)
        w1_hi = [sb(f"w1_hi{i}", [P, KC, F], F32R) for i in range(2)]
        w1_lo = [sb(f"w1_lo{i}", [P, KC, F], F32R) for i in range(2)]
        w2_hi = [sb(f"w2_hi{i}", [P, FC, D], F32R) for i in range(2)]
        w2_lo = [sb(f"w2_lo{i}", [P, FC, D], F32R) for i in range(2)]
        arrived = ctx.enter_context(nc.semaphore("expert_arrived"))
        split = ctx.enter_context(nc.semaphore("expert_split"))
        step = ctx.enter_context(nc.semaphore("expert_step"))
    return Weights


def load_expert(sp, nc, W, io, e):
    if e > 0:
        sp.wait_ge(W.split, e)
    sp.dma_start(W.raw1[:, :, :], io["w1"][e].rearrange("(k p) f -> p k f", p=P)).then_inc(W.arrived, 16)
    sp.dma_start(W.raw2[:, :, :], io["w2"][e].rearrange("(k p) d -> p k d", p=P)).then_inc(W.arrived, 16)


def split_expert(pool, nc, W, e):
    i = e % 2
    pool.wait_ge(W.arrived, 32 * (e + 1))
    nc.gpsimd.tensor_copy(W.w1_hi[i][:, :, :], W.raw1[:, :, :]).then_inc(W.step, 1)
    nc.gpsimd.tensor_copy(W.w2_hi[i][:, :, :], W.raw2[:, :, :]).then_inc(W.step, 1)
    pool.wait_ge(W.step, 2 * (e + 1))
    nc.gpsimd.tensor_tensor(W.w1_lo[i][:, :, :], W.raw1[:, :, :], W.w1_hi[i][:, :, :].bitcast(F32), ALU.subtract)
    nc.gpsimd.tensor_tensor(W.w2_lo[i][:, :, :], W.raw2[:, :, :], W.w2_hi[i][:, :, :].bitcast(F32), ALU.subtract).then_inc(W.split, 1)


def attention_and_router(nc, ctx, io, xt, y2_hi, y2_lo, gates, W, wide, narrow, values):
    def sb(name, shape, dt):
        return ctx.enter_context(nc.sbuf_tensor(name, shape, dt))

    def sem(name):
        return ctx.enter_context(nc.semaphore(name))

    ident = sb("ident2", [P, P], F32)
    wraw = sb("wraw2", [P, KC, QKV], F32)
    qkvw_hi, qkvw_lo = sb("qkvw_hi", [P, KC, QKV], F32R), sb("qkvw_lo", [P, KC, QKV], F32R)
    projw_hi, projw_lo = sb("projw_hi", [P, KC, D], F32R), sb("projw_lo", [P, KC, D], F32R)
    rw_hi, rw_lo = sb("rw_hi", [P, KC, E_], F32R), sb("rw_lo", [P, KC, E_], F32R)
    lncol = sb("lncol", [P, 4, KC], F32)
    iota = sb("iota", [P, E_], F32)
    stats, mv = sb("stats2", [P, NT, 6], F32), sb("mv2", [P, NT, 2], F32)
    varc, std, rstd = sb("varc2", [P, NT], F32), sb("std2", [P, NT], F32), sb("rstd2", [P, NT], F32)
    h0 = sb("h0", [P, NT, D], F32)
    norm = sb("norm", [P, 2, QT, D], F32)
    full = sb("full", [P, KC, 512], F32)
    yT_hi, yT_lo = sb("yT_hi", [P, KC, 512], F32R), sb("yT_lo", [P, KC, 512], F32R)
    qkv = sb("qkv", [P, NT, QKV], F32)
    prod = sb("prod", [P, B, D], F32)
    sc = sb("sc", [P, QT * B, B, H], F32)
    top = sb("top", [P, QT * B * H], F32)
    den = sb("den", [P, QT * B * H], F32)
    ao = sb("ao", [P, NT, D], F32)
    logits = sb("logits", [P, NT, E_], F32)
    lmax = sb("lmax", [P, NT], F32)
    gsum = sb("gsum", [P, NT], F32)
    best = sb("best", [P, NT, 8], F32)
    which = sb("which", [P, NT, 8], mybir.dt.uint32)
    chosen = sb("chosen", [P, NT, E_], F32)

    const_in, wraw_in, w_split = sem("const_in2"), sem("wraw_in2"), sem("w_split2")
    var_set, std_set = sem("var_set2"), sem("std_set2")
    norm_set, transposed, full_set, parts_set = sem("norm_set"), sem("transposed"), sem("full_set"), sem("parts_set")
    product_ready, qkv_copied, added = sem("product_ready"), sem("qkv_copied"), sem("added")
    scores_set, exps_set, ao_set = sem("scores_set"), sem("exps_set"), sem("ao_set")
    logits_ready, shifted, gate_exps = sem("logits_ready"), sem("shifted"), sem("gate_exps")
    residual_set = sem("residual_set")
    x2_set = sem("x2_set")
    dve_step = sem("dve_step2")

    def turn_full(turn):
        return 2 * min(turn + 1, 4) + max(0, min(turn + 1 - 4, 4)) + 2 * max(0, turn + 1 - 8)

    block = ctx.enter_context(nc.Block())
    weights = (("wqkv", wraw[:, :, :], qkvw_hi, qkvw_lo), ("wproj", wraw[:, :, 0:D], projw_hi, projw_lo),
               ("router", wraw[:, :, 0:E_], rw_hi, rw_lo))

    @block.sync
    def _(sp):
        sp.dma_start(ident[:, :], io["ident"]).then_inc(const_in, 16)
        sp.dma_start(lncol[:, :, :], io["lncol"]).then_inc(const_in, 16)
        sp.dma_start(iota[:, :], io["iota"]).then_inc(const_in, 16)
        for n, (name, raw, _, _) in enumerate(weights):
            if n > 0:
                sp.wait_ge(w_split, n)
            sp.dma_start(raw, io[name].rearrange("(k p) n -> p k n", p=P)).then_inc(wraw_in, 16)
        for e in range(2):
            load_expert(sp, nc, W, io, e)

    @block.gpsimd
    def _(pool):
        for e in range(2):
            split_expert(pool, nc, W, e)
        pool.wait_ge(x2_set, 1)
        nc.gpsimd.tensor_tensor(xt[:, :, :], xt[:, :, :], h0[:, :, :], ALU.add).then_inc(residual_set, 1)

    @block.scalar
    def _(act):
        def roots(k):
            act.wait_ge(var_set, k + 1)
            nc.scalar.activation(std[:, :], varc[:, :], ACT.Sqrt).then_inc(std_set, 1)

        def apply_affine(turn):
            which_norm = 0 if turn < 4 else 1
            act.wait_ge(transposed, turn + 1)
            if turn > 0:
                act.wait_ge(parts_set, turn)
            for k in range(KC):
                nc.scalar.activation(full[:, k, :], wide[turn % 2][:, k, :], ACT.Identity,
                                     scale=lncol[:, 2 * which_norm, k:k + 1], bias=lncol[:, 2 * which_norm + 1, k:k + 1]).then_inc(full_set, 1)

        roots(0)
        roots(1)
        act.wait_ge(const_in, 48)
        for s in range(B):
            apply_affine(s)
            for t in range(QT):
                i = QT * s + t
                act.wait_ge(product_ready, i + 1)
                nc.scalar.activation(qkv[:, i, :], narrow[i % 3][:, 0:QKV], ACT.Copy).then_inc(qkv_copied, 1)
        act.wait_ge(scores_set, 1)
        nc.scalar.activation(sc[:, :, :, :], sc[:, :, :, :], ACT.Exp, scale=DK ** -0.5).then_inc(exps_set, 1)
        for s in range(B):
            act.wait_ge(transposed, 4 + s + 1)
            if s > 0:
                act.wait_ge(product_ready, NT + QT * s)
            nc.scalar.activation(yT_hi[:, :, :], wide[s % 2][:, :, :], ACT.Copy).then_inc(full_set, 1)
        roots(2)
        for s in range(B):
            apply_affine(8 + s)
        act.wait_ge(shifted, 1)
        nc.scalar.activation(logits[:, :, :], logits[:, :, :], ACT.Exp).then_inc(gate_exps, 1)

    @block.vector
    def _(dve):
        steps = [0]

        def step(ins):
            steps[0] += 1
            ins.then_inc(dve_step, 1)

        def settle():
            dve.wait_ge(dve_step, steps[0])

        def statistics(k, src):
            for t in range(NT):
                step(nc.vector.bn_stats(stats[:, t, :], src[:, t, :]))
            settle()
            for t in range(NT):
                step(nc.vector.bn_aggr(mv[:, t, :], stats[:, t, :]))
            settle()
            nc.vector.tensor_scalar_add(varc[:, :], mv[:, :, 1], EPS).then_inc(var_set, 1)
            dve.wait_ge(std_set, k + 1)
            step(nc.vector.reciprocal(rstd[:, :], std[:, :]))
            settle()

        def normalise(dst, src, t):
            return nc.vector.tensor_scalar(dst, src, mv[:, t, 0:1], rstd[:, t:t + 1], ALU.subtract, ALU.mult)

        def normalise_turn(turn):
            if turn >= 10 or turn in (2, 3):
                dve.wait_ge(transposed, turn - 1)
            for t in range(QT):
                i = QT * (turn % 4) + t
                last = normalise(norm[:, turn % 2, t, :], h0[:, i, :], i)
            last.then_inc(norm_set, 1)

        def split_turn(turn, hi, lo):
            if turn < 8 and turn % 4 > 0:
                dve.wait_ge(product_ready, NT * (turn // 4) + QT * (turn % 4))
            dve.wait_ge(full_set, turn_full(turn))
            step(nc.vector.tensor_copy(hi, full[:, :, :]))
            settle()
            nc.vector.tensor_tensor(lo, full[:, :, :], hi.bitcast(F32), ALU.subtract).then_inc(parts_set, 1)

        for n, (_, raw, hi, lo) in enumerate(weights):
            dve.wait_ge(wraw_in, 16 * (n + 1))
            step(nc.vector.tensor_copy(hi[:, :, :], raw))
            settle()
            nc.vector.tensor_tensor(lo[:, :, :], raw, hi[:, :, :].bitcast(F32), ALU.subtract).then_inc(w_split, 1)
        step(nc.vector.memset(sc[:, :, :, :], LEAST))
        statistics(0, xt)
        for t in range(NT):
            step(normalise(h0[:, t, :], xt[:, t, :], t))
        settle()
        statistics(1, h0)
        normalise_turn(0)
        normalise_turn(1)
        for s in range(B):
            split_turn(s, yT_hi[:, :, :], yT_lo[:, :, :])
            if s + 2 < B:
                normalise_turn(s + 2)

        def head_dims(i, a):
            return qkv[:, i, a:a + D].rearrange("p (g r d) -> p g r d", g=EH, r=REP)

        def shared(i, a):
            return qkv[:, i, a:a + EH * DK].rearrange("p (g r d) -> p g r d", g=EH, r=1).to_broadcast([P, EH, REP, DK])

        dve.wait_ge(qkv_copied, NT)
        for j in range(QT):
            for s in range(B):
                if j + s > 0:
                    settle()
                for t in range(s + 1):
                    step(nc.vector.tensor_tensor(prod[:, t, :].rearrange("p (g r d) -> p g r d", g=EH, r=REP),
                                                 head_dims(QT * s + j, 0), shared(QT * t + j, D), ALU.mult))
                settle()
                step(nc.vector.tensor_reduce(sc[:, B * j + s, 0:s + 1, :], prod[:, 0:s + 1, :].rearrange("p t (h d) -> p t h d", h=H),
                                             axis=AX.X, op=ALU.add))
        settle()
        by_head = sc[:, :, :, :].rearrange("p a t h -> p a h t")
        topv = top[:, :].rearrange("p (a h) -> p a h", h=H)
        denv = den[:, :].rearrange("p (a h) -> p a h", h=H)
        step(nc.vector.tensor_reduce(topv, by_head, axis=AX.X, op=ALU.max))
        settle()
        nc.vector.tensor_tensor(sc[:, :, :, :], sc[:, :, :, :], topv.unsqueeze(2).to_broadcast([P, QT * B, B, H]), ALU.subtract).then_inc(scores_set, 1)
        dve.wait_ge(exps_set, 1)
        step(nc.vector.tensor_reduce(denv, by_head, axis=AX.X, op=ALU.add))
        settle()
        step(nc.vector.reciprocal(top[:, :], den[:, :]))
        settle()
        step(nc.vector.tensor_tensor(sc[:, :, :, :], sc[:, :, :, :], topv.unsqueeze(2).to_broadcast([P, QT * B, B, H]), ALU.mult))
        for j in range(QT):
            for s in range(B):
                settle()
                for t in range(s + 1):
                    pr = sc[:, B * j + s, t, :].rearrange("p (g r d) -> p g r d", g=EH, d=1).to_broadcast([P, EH, REP, DK])
                    step(nc.vector.tensor_tensor(prod[:, t, :].rearrange("p (g r d) -> p g r d", g=EH, r=REP),
                                                 pr, shared(QT * t + j, D + EH * DK), ALU.mult))
                settle()
                out = ao[:, QT * s + j, :]
                if s == 0:
                    last = nc.vector.tensor_copy(out, prod[:, 0, :])
                else:
                    last = nc.vector.tensor_reduce(out, prod[:, 0:s + 1, :].rearrange("p t c -> p c t"), axis=AX.X, op=ALU.add)
                step(last)
        settle()
        nc.vector.nop().then_inc(ao_set, 1)
        for s in range(B):
            dve.wait_ge(full_set, turn_full(4 + s))
            nc.vector.tensor_tensor(yT_lo[:, :, :], wide[s % 2][:, :, :], yT_hi[:, :, :].bitcast(F32), ALU.subtract).then_inc(parts_set, 1)
            for t in range(QT):
                i = QT * s + t
                dve.wait_ge(product_ready, NT + i + 1)
                nc.vector.tensor_tensor(h0[:, i, :], narrow[(NT + i) % 3][:, 0:D], h0[:, i, :], ALU.add).then_inc(added, 1)
        dve.wait_ge(added, NT)
        nc.vector.nop().then_inc(x2_set, 1)
        statistics(2, h0)
        normalise_turn(8)
        normalise_turn(9)
        for s in range(B):
            part = slice(512 * s, 512 * s + 512)
            split_turn(8 + s, y2_hi[:, :, part], y2_lo[:, :, part])
            if s + 2 < B:
                normalise_turn(8 + s + 2)

        def per_tile(a):
            return a.unsqueeze(2).to_broadcast([P, NT, E_])

        dve.wait_ge(logits_ready, 1)
        lv = values[:, 0:NT * E_].rearrange("p (t e) -> p t e", e=E_)
        step(nc.vector.tensor_reduce(lmax[:, :], lv, axis=AX.X, op=ALU.max))
        settle()
        nc.vector.tensor_tensor(logits[:, :, :], lv, per_tile(lmax[:, :]), ALU.subtract).then_inc(shifted, 1)
        dve.wait_ge(gate_exps, 1)
        step(nc.vector.tensor_reduce(gsum[:, :], logits[:, :, :], axis=AX.X, op=ALU.add))
        settle()
        step(nc.vector.reciprocal(lmax[:, :], gsum[:, :]))
        settle()
        step(nc.vector.tensor_tensor(logits[:, :, :], logits[:, :, :], per_tile(lmax[:, :]), ALU.mult))
        settle()
        for t in range(NT):
            step(nc.vector.max(best[:, t, :], logits[:, t, :]))
        settle()
        for t in range(NT):
            step(nc.vector.max_index(which[:, t, :], best[:, t, :], logits[:, t, :]))
        settle()
        numbers = iota[:, :].unsqueeze(1).to_broadcast([P, NT, E_])
        for i, dst in ((0, gates), (1, chosen)):
            step(nc.vector.tensor_tensor(dst[:, :, :], numbers, per_tile(which[:, :, i]), ALU.is_equal))
            settle()
            step(nc.vector.tensor_tensor(dst[:, :, :], dst[:, :, :], per_tile(best[:, :, i]), ALU.mult))
            settle()
        step(nc.vector.tensor_tensor(gates[:, :, :], gates[:, :, :], chosen[:, :, :], ALU.add))
        settle()

    @block.tensor
    def _(pe):
        pe.wait_ge(const_in, 48)

        def transposes(turn, src):
            if turn >= 2:
                pe.wait_ge(parts_set, turn - 1)
            for k in range(KC):
                for t in range(QT):
                    last = nc.tensor.transpose(wide[turn % 2][:, k, P * t:P * t + P], src(t)[:, P * k:P * k + P], ident[:, :])
            last.then_inc(transposed, 1)

        def products(out, hi, lo, t, w_hi, w_lo):
            for i, (a, c) in enumerate(((hi, w_hi), (hi, w_lo), (lo, w_hi))):
                for k in range(KC):
                    last = nc.tensor.matmul(out, a[:, k, P * t:P * t + P], c[:, k, :], start=(i, k) == (0, 0), stop=(i, k) == (2, KC - 1))
            return last

        def first_turn(s):
            pe.wait_ge(norm_set, s + 1)
            transposes(s, lambda t: norm[:, s % 2, t, :])

        first_turn(0)
        for s in range(B):
            if s + 1 < B:
                first_turn(s + 1)
            pe.wait_ge(parts_set, s + 1)
            pe.wait_ge(w_split, 1)
            for t in range(QT):
                i = QT * s + t
                if i >= 3:
                    pe.wait_ge(qkv_copied, i - 2)
                products(narrow[i % 3][:, 0:QKV], yT_hi, yT_lo, t, qkvw_hi, qkvw_lo).then_inc(product_ready, 1)
        pe.wait_ge(ao_set, 1)
        pe.wait_ge(w_split, 2)
        transposes(4, lambda t: ao[:, t, :])
        for s in range(B):
            if s + 1 < B:
                transposes(4 + s + 1, lambda t: ao[:, QT * (s + 1) + t, :])
            pe.wait_ge(parts_set, 4 + s + 1)
            for t in range(QT):
                i = QT * s + t
                if i >= 3:
                    pe.wait_ge(added, i - 2)
                products(narrow[(NT + i) % 3][:, 0:D], yT_hi, yT_lo, t, projw_hi, projw_lo).then_inc(product_ready, 1)

        def last_turn(s):
            pe.wait_ge(norm_set, 4 + s + 1)
            transposes(8 + s, lambda t: norm[:, s % 2, t, :])

        last_turn(0)
        pe.wait_ge(w_split, 3)
        for s in range(B):
            if s + 1 < B:
                last_turn(s + 1)
            pe.wait_ge(parts_set, 8 + s + 1)
            for t in range(QT):
                i = QT * s + t
                last = products(values[:, E_ * i:E_ * i + E_], y2_hi, y2_lo, i, rw_hi, rw_lo)
        last.then_inc(logits_ready, 1)


def experts(nc, ctx, io, xt, y2_hi, y2_lo, gates, W, wide, narrow, values, out):
    def sb(name, shape, dt):
        return ctx.enter_context(nc.sbuf_tensor(name, shape, dt))

    def sem(name):
        return ctx.enter_context(nc.semaphore(name))

    CH = 512
    NCH = NT * P // CH
    TC = CH // P
    chunks = E_ * NCH
    hid = [sb(f"hid{i}", [P, FC, CH], F32) for i in range(2)]
    hid_hi = [sb(f"hid_hi{i}", [P, FC, CH], F32R) for i in range(2)]
    hid_lo = [sb(f"hid_lo{i}", [P, FC, CH], F32R) for i in range(2)]
    up_banks = [wide[f // 2][:, f % 2, :] for f in range(FC)]
    down_banks = [narrow[0], narrow[1], narrow[2], values]
    up_ready, gelu_done, hi_set, parts_set = sem("up_ready"), sem("gelu_done"), sem("hid_hi_set"), sem("hid_parts_set")
    down_ready, summed, stored = sem("down_ready"), sem("summed"), sem("stored")

    block = ctx.enter_context(nc.Block())

    @block.sync
    def _(sp):
        for e in range(2, E_):
            load_expert(sp, nc, W, io, e)
        for c in range(NCH):
            sp.wait_ge(summed, TC * (chunks - NCH + c + 1))
            sp.dma_start(out[CH * c:CH * c + CH, :].rearrange("(t p) d -> p t d", p=P), xt[:, TC * c:TC * c + TC, :]).then_inc(stored, 16)
        sp.wait_ge(stored, 16 * NCH)

    @block.gpsimd
    def _(pool):
        for e in range(2, E_):
            pool.wait_ge(down_ready, TC * NCH * (e - 1))
            split_expert(pool, nc, W, e)

    @block.scalar
    def _(act):
        for m in range(chunks):
            for f in range(FC):
                act.wait_ge(up_ready, FC * m + f + 1)
                if m >= 2:
                    act.wait_ge(parts_set, FC * (m - 2) + f + 1)
                nc.scalar.activation(hid[m % 2][:, f, :], up_banks[f], ACT.Gelu_apprx_tanh).then_inc(gelu_done, 1)

    @block.vector
    def _(dve):
        def split(m):
            i = m % 2
            if m >= 2:
                dve.wait_ge(down_ready, TC * (m - 1))
            for f in range(FC):
                dve.wait_ge(gelu_done, FC * m + f + 1)
                nc.vector.tensor_copy(hid_hi[i][:, f, :], hid[i][:, f, :]).then_inc(hi_set, 1)
            for f in range(FC):
                dve.wait_ge(hi_set, FC * m + f + 1)
                nc.vector.tensor_tensor(hid_lo[i][:, f, :], hid[i][:, f, :], hid_hi[i][:, f, :].bitcast(F32), ALU.subtract).then_inc(parts_set, 1)

        split(0)
        for m in range(chunks):
            if m + 1 < chunks:
                split(m + 1)
            e, c = divmod(m, NCH)
            for j in range(TC):
                t = TC * c + j
                dve.wait_ge(down_ready, TC * m + j + 1)
                if e > 0:
                    dve.wait_ge(summed, TC * (m - NCH) + j + 1)
                nc.vector.scalar_tensor_tensor(out=xt[:, t, :], in0=down_banks[j][:, 0:D], scalar=gates[:, t, e:e + 1],
                                               in1=xt[:, t, :], op0=ALU.mult, op1=ALU.add).then_inc(summed, 1)

    @block.tensor
    def _(pe):
        def up(m):
            e, c = divmod(m, NCH)
            if c == 0:
                pe.wait_ge(W.split, e + 1)
            cols = slice(CH * c, CH * c + CH)
            for f in range(FC):
                rows = slice(P * f, P * f + P)
                if m >= 1:
                    pe.wait_ge(gelu_done, FC * (m - 1) + f + 1)
                for i, (w, y) in enumerate(((W.w1_hi, y2_hi), (W.w1_hi, y2_lo), (W.w1_lo, y2_hi))):
                    for k in range(KC):
                        last = nc.tensor.matmul(up_banks[f], w[e % 2][:, k, rows], y[:, k, cols], start=(i, k) == (0, 0), stop=(i, k) == (2, KC - 1))
                last.then_inc(up_ready, 1)

        def down(m):
            e, i = m // NCH, m % 2
            pe.wait_ge(parts_set, FC * (m + 1))
            for j in range(TC):
                toks = slice(P * j, P * j + P)
                if m >= 1:
                    pe.wait_ge(summed, TC * (m - 1) + j + 1)
                n = 0
                for h, w in ((hid_hi, W.w2_hi), (hid_hi, W.w2_lo), (hid_lo, W.w2_hi)):
                    for f in range(FC):
                        last = nc.tensor.matmul(down_banks[j][:, 0:D], h[i][:, f, toks], w[e % 2][:, f, :], start=n == 0, stop=n == 3 * FC - 1)
                        n += 1
                last.then_inc(down_ready, 1)

        up(0)
        for m in range(chunks):
            if m + 1 < chunks:
                up(m + 1)
            down(m)


def tables():
    inv = 1.0 / np.float32(10000.0) ** (np.arange(0, DK, 2, dtype=np.float32) / DK)
    ang = np.repeat(np.arange(SK, dtype=np.float32)[:, None] * inv.astype(np.float32)[None, :], 2, axis=-1)
    sign = np.where(np.arange(DK) % 2 == 0, -1.0, 1.0).astype(np.float32)
    c, s = (np.tile(v, (1, CD // DK)).reshape(KT, P, CD).transpose(1, 0, 2) for v in (np.cos(ang), np.sin(ang) * sign))
    return {"cos": np.ascontiguousarray(c), "sin": np.ascontiguousarray(s), "ident": np.eye(P, dtype=np.float32),
            "iota": np.tile(np.arange(E_, dtype=np.float32), (P, 1)),
            "mask_coef": np.tile(np.array(MASK_PARTS, np.float32), B)[:, None]}


def program(nc, io, out):
    with ExitStack() as ctx:
        xt = ctx.enter_context(nc.sbuf_tensor("xt", [P, NT, D], F32))
        wide = [ctx.enter_context(nc.psum_tensor(f"wide{i}", [P, 2, 512], F32)) for i in range(2)]
        narrow = [ctx.enter_context(nc.psum_tensor(f"narrow{i}", [P, 512], F32)) for i in range(3)]
        values = ctx.enter_context(nc.psum_tensor("values", [P, 512], F32))
        with ExitStack() as part:
            cross_attention(nc, part, io, xt, wide, narrow, values)
        y2_hi = ctx.enter_context(nc.sbuf_tensor("y2_hi", [P, KC, NT * P], F32R))
        y2_lo = ctx.enter_context(nc.sbuf_tensor("y2_lo", [P, KC, NT * P], F32R))
        gates = ctx.enter_context(nc.sbuf_tensor("gates", [P, NT, E_], F32))
        W = expert_weights(nc, ctx, io)
        with ExitStack() as part:
            attention_and_router(nc, part, io, xt, y2_hi, y2_lo, gates, W, wide, narrow, values)
        with ExitStack() as part:
            experts(nc, part, io, xt, y2_hi, y2_lo, gates, W, wide, narrow, values, out)


def kernel(**inputs):
    import concourse.bacc as _bacc
    from concourse.bass_utils import run_bass_kernel_spmd as _run

    a = {k: np.asarray(v) for k, v in inputs.items()}
    T = np.ascontiguousarray
    arrays = {
        "x": T(a["x"].reshape(B * SQ, D)),
        "ctxT": T(a["ctx_1024"].reshape(B * SK, D).T),
        "mask_col": T(a["mask_BxS2_ik0"].reshape(B * KT, P).T),
        "mask_row": T(np.repeat(a["mask_BxS2_ik0"], 2, axis=0)),
        **{"w" + w: T(a["L0_xattn_w_" + w].reshape(2, HH, DK, D).transpose(3, 0, 2, 1).reshape(D, D)) for w in "qk"},
        **{"w" + w: T(a["L0_xattn_w_" + w].T) for w in "vo"},
        "wqkv": T(a["L0_ffn_qkv_weight"].T),
        "wproj": T(a["L0_ffn_proj_weight"].T),
        "router": T(a["L0_ffn_router_weight"].T),
        "w1": T(a["L0_ffn_moe_w1"]),
        "w2": T(a["L0_ffn_moe_w2"]),
        "lncol": T(np.stack([a["L0_ffn_ln1_weight"], a["L0_ffn_ln1_bias"], a["L0_ffn_ln2_weight"],
                             a["L0_ffn_ln2_bias"]]).reshape(4, KC, P).transpose(2, 0, 1)),
        **tables(),
    }
    nc = _bacc.Bacc("TRN2", target_bir_lowering=False, num_devices=1)
    io = {n: nc.dram_tensor("in_" + n, v.shape, mybir.dt.from_np(v.dtype), kind="ExternalInput").ap() for n, v in arrays.items()}
    out = nc.dram_tensor("out", (B * SQ, D), F32, kind="ExternalOutput").ap()
    program(nc, io, out)
    r = _run(nc, [{"in_" + n: v for n, v in arrays.items()}], core_ids=[0])
    return r.results[0]["out"].reshape(B, SQ, D)
```

```python
import numpy as np
import concourse.bass as bass
from concourse import mybir
from contextlib import ExitStack

F32 = mybir.dt.float32
F32R = mybir.dt.float32r
BF16 = mybir.dt.bfloat16
I32 = mybir.dt.int32
ALU = mybir.AluOpType
ACT = mybir.ActivationFunctionType
AX = mybir.AxisListType

P = 128
B, SQ, SK, D = 4, 512, 1024, 256
H, DK = 16, 16
KC = D // P
QT, KT = SQ // P, SK // P
NT = B * QT
EPS = 1e-5
MASKED = -10000.0
HH = H // 2
UNITS = 2 * B
CD = D // HH
QUADS = 2 * UNITS
GROUPS = QUADS * KT
PIECE_RUNS = ((0, 3), (1, 2), (2, 1))
R_MASK = sum(n for _, n in PIECE_RUNS) * DK
R_MAX = R_MASK + 2
R_ALL = R_MAX + 3
MASK_PARTS = (-39936.0, -64.0)
assert sum(MASK_PARTS) == MASKED * DK ** 0.5


def attention_jobs():
    def proj(b):
        jobs = [("xT", b)] + [("q", b, j) for j in range(QT)] + [("trq", b)]
        for g in range(2):
            jobs += [("kv", b, g * 4 + j) for j in range(4)] + [("trk", b, g)]
        return jobs

    def maxes(quad):
        return [("max", quad, h, qt) for h in range(4) for qt in range(QT)] + [("mxt", quad)]

    def interleave(many, few):
        out, n = [], 0
        for i, j in enumerate(many):
            out.append(j)
            while n < len(few) and (n + 1) * len(many) <= (i + 1) * len(few):
                out.append(few[n])
                n += 1
        return out + few[n:]

    cost = {"xT": 1.55, "q": 0.77, "kv": 0.67, "trq": 3.2, "trk": 2.3, "max": 1.13, "mxt": 2}
    before = proj(0) + proj(1)[:EARLY] + maxes(0)
    places = [[] for _ in range(GROUPS)]
    for b in range(B):
        work = sum((maxes(4 * b + i) for i in range(1, 5 if b + 1 < B else 4)), [])
        if b == 0:
            work = work[:18] + interleave(work[18:37], proj(1)[EARLY:]) + work[37:]
        elif b + 1 < B:
            work = work[:22] + interleave(work[22:39], proj(b + 1)[1:]) + work[39:]
        first = max(32 * b - LEAD, 0)
        last = 32 * b + 32 - LEAD if b + 1 < B else GROUPS - 8 - LEAD
        total, spent = sum(cost[j[0]] for j in work), 0.0
        for j in work:
            places[first + int(spent / total * (last - first))].append(j)
            spent += cost[j[0]]
    for quad in range(QUADS - 1):
        places[8 * quad + 9].insert(1, ("out", quad))
    for b in range(B - 1):
        if b > 0:
            places[32 * b + 4].insert(0, ("xT", b + 1))
        places[32 * b + 34].insert(2, ("oT", b))
        places[32 * b + 35].insert(1, ("oP", b))
    after = [("out", QUADS - 1), ("oT", B - 1), ("oP", B - 1)]
    jobs = before + [j for now in places for j in now] + after
    index = {j: n for n, j in enumerate(jobs)}
    for b in range(B - 1):
        assert index[("oT", b)] < index[("oP", b)] < index.get(("xT", b + 2), len(jobs))
        assert index.get(("oP", b - 1), -1) < index[("xT", b + 1)] < index[("q", b + 1, 0)]
        assert index[("xT", b + 1)] < index[("out", 4 * b)]
    return index, before, places, after


EARLY = 11
GROUP_STEPS = (("score", 0), ("score", 1), ("jobs", slice(0, 1)), ("score", 2), ("weigh", 0), ("jobs", slice(1, 2)),
               ("score", 3), ("jobs", slice(2, None)))
LEAD = 4


def cross_attention(nc, ctx, io, xt, wide, narrow, values):
    index, before, places, after = attention_jobs()
    jobs = sorted(index, key=index.get)

    def sb(name, shape, dt):
        return ctx.enter_context(nc.sbuf_tensor(name, shape, dt))

    def sem(name):
        return ctx.enter_context(nc.semaphore(name))

    ident = sb("ident", [P, P], F32)
    w_hi = {w: sb(f"w{w}_hi", [P, KC, D], F32R) for w in "qkvo"}
    w_lo = {w: sb(f"w{w}_lo", [P, KC, D], F32R) for w in "qkvo"}
    cos = sb("cos", [P, KT, CD], F32)
    sin = sb("sin", [P, KT, CD], F32)
    mcol_i = sb("mcol_i", [P, B * KT], I32)
    mcol = sb("mcol", [P, B * KT], F32)
    kcos = sb("kcos", [P, 2, KT, CD], F32)
    ksin = sb("ksin", [P, 2, KT, CD], F32)
    mcoef = sb("mcoef", [2 * B, 1], F32)
    mrow = sb("mrow", [2 * B, SK], BF16)
    stats = sb("stats", [P, NT, 6], F32)
    mv = sb("mv", [P, NT, 2], F32)
    varc = sb("varc", [P, NT], F32)
    std = sb("std", [P, NT], F32)
    rstd = sb("rstd", [P, NT], F32)
    xT_hi = sb("xT_hi", [P, KC, SQ], F32R)
    xT_lo = sb("xT_lo", [P, KC, SQ], F32R)
    craw = sb("craw", [P, KC, 512], F32)
    c_hi = sb("c_hi", [P, KC, SK], F32R)
    c_lo = sb("c_lo", [P, KC, SK], F32R)
    rope_b = sb("rope_b", [P, 2, D], F32)
    roped = sb("roped", [P, 8, D], F32)
    pieces = sb("pieces", [P, 2, 3, KC, 512], BF16)
    rest = sb("rest", [P, KC, 512], F32)
    qst = [sb(f"qst{i}", [R_ALL, HH, SQ], BF16) for i in range(3)]
    kst = [sb(f"kst{i}", [R_ALL, HH, SK], BF16) for i in range(3)]
    mx = [sb(f"mx{i}", [P, QT * 4], F32) for i in range(2)]
    mxp = sb("mxp", [4, 3, SQ], BF16)
    vaug = [sb(f"vaug{i}", [P, KT, H, DK + 1], F32) for i in range(2)]
    NP = 7
    probs = sb("probs", [P, NP, SQ], F32)
    wraw = {w: probs[:, n, :].rearrange("p (k d) -> p k d", k=KC) for n, w in enumerate("qkvo")}
    mrow_i = probs[0:2 * B, 4:6, :].rearrange("r a n -> r (a n)").bitcast(I32)
    ones = probs[0:8, 6, 0:256].bitcast(BF16)
    outT = sb("outT", [P, SQ], F32)
    rec = sb("rec", [P, 16], F32)
    attn = sb("attn", [P, QT, D], F32)
    xn = attn
    aT_hi, aT_lo = xT_hi, xT_lo
    q_dram = nc.dram_tensor("q_pieces", [B, 3, KC, P, SQ], BF16, kind="Internal").ap()
    m_dram = nc.dram_tensor("m_pieces", [QUADS, 4, 3, SQ], BF16, kind="Internal").ap()
    k_dram = nc.dram_tensor("k_pieces", [B, 3, KC, P, SK], BF16, kind="Internal").ap()

    x_in = [sem(f"x_in{b}") for b in range(B)]
    w_in = {w: sem(f"w{w}_in") for w in "qkvo"}
    tab_in, c_in = sem("tab_in"), sem("c_in")
    ones_set, ones_in = sem("ones_set"), sem("ones_in")
    stack_in = [sem(f"stack_in{i}") for i in range(3)]
    maxrow_in, maxrow_out = [sem(f"maxrow_in{i}") for i in range(2)], sem("maxrow_out")
    pieces_out = [sem(f"pieces_out{i}") for i in range(2)]
    w_split, c_high, c_split, mask_set = sem("w_split"), sem("c_high"), sem("c_split"), sem("mask_set")
    var_set, std_set, xn_set, values_prepared = sem("var_set"), sem("std_set"), sem("xn_set"), sem("values_prepared")
    dve_step = sem("dve_step")
    pe_done, dve_done, act_done, pool_done = sem("pe_done"), sem("dve_done"), sem("act_done"), sem("pool_done")
    score_ready, exp_done, pv_done, outT_set = sem("score_ready"), sem("exp_done"), sem("pv_done"), sem("outT_set")

    STACK = 16 * (2 * len(PIECE_RUNS) + 1)
    SPLIT = ("xT", "trq", "trk", "mxt", "oT")
    ACT_KINDS = SPLIT + ("kv",)
    POOL_KINDS = ("q", "kv", "trq", "trk")
    PIECED = ("trq", "trk")

    def act_count(n):
        return sum(j[0] in ACT_KINDS for j in jobs[:n + 1])

    def pool_count(n):
        return sum(j[0] in POOL_KINDS for j in jobs[:n + 1])

    def last_before(n, kinds):
        return max((m for m in range(n) if jobs[m][0] in kinds), default=-1)

    high_context = {("kv", 0, 0): 1, ("trk", 0, 0): 2, ("trk", 0, 1): 3, ("mxt", 1): 4, ("mxt", 2): 5, ("trk", 2, 1): 6, ("mxt", 8): 7}
    assert sorted(high_context, key=index.get) == list(high_context) and len(high_context) == 2 * B - 1
    assert all(index[j] < index[("kv", i // 2, 4 * (i % 2))] for j, i in high_context.items())

    def tile_number(j):
        return j[1] * (QT + KT) + (j[2] if j[0] == "q" else QT + j[2])

    def transposed_by(tile):
        b, r = divmod(tile, QT + KT)
        return index[("trq", b) if r < QT else ("trk", b, (r - QT) // 4)]

    def piece_job(j):
        return 3 * j[1] + (0 if j[0] == "trq" else 1 + j[2])

    def pieces_stored(last, i):
        return sum(t % 2 == i for t in range(last + 1))

    block = ctx.enter_context(nc.Block())

    @block.sync
    def _(sp):
        def load_x(b):
            sp.dma_start(xt[:, QT * b:QT * b + QT, :],
                         io["x"][SQ * b:SQ * b + SQ, :].rearrange("(t p) d -> p t d", p=P)).then_inc(x_in[b], 16)

        def load_context(i):
            if i > 0:
                sp.wait_ge(c_split, i)
            sp.dma_start(craw[:, :, :], io["ctxT"][:, 512 * i:512 * i + 512].rearrange("(k p) t -> p k t", p=P)).then_inc(c_in, 16)

        def load_stack(u):
            b, c = divmod(u, 2)
            if u >= 3:
                sp.wait_ge(score_ready, 64 * (u - 2))
            row = 0
            for piece, n in PIECE_RUNS:
                rows = slice(row, row + DK * n)
                sp.dma_start(qst[u % 3][rows, :, :].rearrange("r h t -> r (h t)"),
                             q_dram[b, piece, c].rearrange("(d h) t -> d (h t)", h=HH)
                             .unsqueeze(0).to_broadcast([n, DK, HH * SQ])).then_inc(stack_in[u % 3], 16)
                sp.dma_start(kst[u % 3][rows, :, :].rearrange("r h t -> r (h t)"),
                             k_dram[b, 0:n, c].rearrange("a (d h) t -> a d (h t)", h=HH)).then_inc(stack_in[u % 3], 16)
                row += DK * n
            sp.dma_start(kst[u % 3][R_MASK:R_MAX, :, :],
                         mrow[2 * b:2 * b + 2, :].unsqueeze(1).to_broadcast([2, HH, SK])).then_inc(stack_in[u % 3], 16)

        def load_max_rows(quad):
            u, h = quad // 2, 4 * (quad % 2)
            sp.wait_ge(dve_done, index[("mxt", quad)] + 1)
            sp.dma_start(m_dram[quad], mxp[:, :, :]).then_inc(maxrow_out, 16)
            sp.wait_ge(maxrow_out, 16 * (quad + 1))
            if quad >= 2:
                sp.wait_ge(score_ready, 32 * (quad - 2) + 1)
            sp.dma_start(qst[u % 3][R_MAX:R_ALL, h:h + 4, :], m_dram[quad].rearrange("h a t -> a h t")).then_inc(maxrow_in[quad % 2], 16)

        def store_pieces(j):
            sp.wait_ge(pool_done, pool_count(index[j]))
            dst = q_dram[j[1]] if j[0] == "trq" else k_dram[j[1]][:, :, :, 512 * j[2]:512 * j[2] + 512]
            sp.dma_start(dst.rearrange("a c p t -> p (a c) t"),
                         pieces[:, piece_job(j) % 2, :, :, :].rearrange("p a c t -> p (a c) t")).then_inc(pieces_out[piece_job(j) % 2], 16)

        def batch_stored(b):
            for i in range(2):
                sp.wait_ge(pieces_out[i], 16 * pieces_stored(3 * b + 2, i))

        load_x(0)
        load_context(0)
        for dst, name in ((ident[:, :], "ident"), (mcol_i[:, :], "mask_col"), (mrow_i, "mask_row"), (mcoef[:, :], "mask_coef")):
            sp.dma_start(dst, io[name]).then_inc(tab_in, 16)
        sp.dma_start(cos[:, :, :], io["cos"]).then_inc(tab_in, 16)
        sp.dma_start(sin[:, :, :], io["sin"]).then_inc(tab_in, 16)
        for b in range(1, B):
            load_x(b)
        load_context(1)
        load_context(2)
        sp.wait_ge(ones_in, 6 * 16)
        sp.wait_ge(mask_set, 1)
        store_pieces(("trq", 0))
        store_pieces(("trk", 0, 0))
        load_context(3)
        store_pieces(("trk", 0, 1))
        batch_stored(0)
        load_stack(0)
        load_stack(1)
        store_pieces(("trq", 1))
        store_pieces(("trk", 1, 0))
        load_context(4)
        load_max_rows(0)
        for b in range(B):
            load_max_rows(4 * b + 1)
            if b == 0:
                load_context(5)
            load_max_rows(4 * b + 2)
            if b == 0:
                store_pieces(("trk", 1, 1))
                load_context(6)
                batch_stored(1)
                load_stack(2)
            elif b + 1 < B:
                store_pieces(("trq", b + 1))
                store_pieces(("trk", b + 1, 0))
                store_pieces(("trk", b + 1, 1))
                batch_stored(b + 1)
                load_stack(2 * b + 2)
                if b == 1:
                    load_context(7)
            load_max_rows(4 * b + 3)
            if b + 1 < B:
                load_stack(2 * b + 3)
                load_max_rows(4 * b + 4)

    @block.gpsimd
    def _(pool):
        nc.gpsimd.memset(ones[:, :], 1.0).then_inc(ones_set, 1)

        for i in range(3):
            for st, n in ((qst[i], HH), (kst[i], 2 * HH)):
                pool.wait_ge(ones_set, 1)
                pool.dma_start(st[R_MASK:R_ALL, :, :].rearrange("r h (a n) -> r (h a) n", n=512),
                               ones[0:R_ALL - R_MASK, :].unsqueeze(1).to_broadcast([R_ALL - R_MASK, n, 512])).then_inc(ones_in, 16)

        def split_context(i):
            part = slice(512 * (i % 2), 512 * (i % 2) + 512)
            pool.wait_ge(c_high, i + 1)
            nc.gpsimd.tensor_tensor(c_lo[:, :, part], craw[:, :, :], c_hi[:, :, part].bitcast(F32), ALU.subtract).then_inc(c_split, 1)

        for i in range(2):
            nc.gpsimd.memset(vaug[i][:, :, :, DK:DK + 1], 1.0).then_inc(values_prepared, 1)
        split_context(0)

        def job(j):
            n, kind = index[j], j[0]
            if kind not in POOL_KINDS:
                if j in high_context:
                    split_context(high_context[j])
                return
            pool.wait_ge(dve_done, n + 1)
            if kind in ("q", "kv"):
                r = tile_number(j)
                nc.gpsimd.tensor_tensor(roped[:, r % 8, :], roped[:, r % 8, :], rope_b[:, r % 2, :], ALU.add).then_inc(pool_done, 1)
            else:
                i = piece_job(j) % 2
                nc.gpsimd.tensor_tensor(pieces[:, i, 2, :, :], rest[:, :, :], pieces[:, i, 1, :, :], ALU.subtract).then_inc(pool_done, 1)
            if j in high_context:
                split_context(high_context[j])

        for j in jobs:
            job(j)

    @block.scalar
    def _(act):
        for w in "qkvo":
            act.dma_start(wraw[w], io["w" + w].rearrange("(k p) n -> p k n", p=P)).then_inc(w_in[w], 16)
        def deviation(i, tiles):
            act.wait_ge(var_set, i + 1)
            nc.scalar.activation(std[:, tiles], varc[:, tiles], ACT.Sqrt).then_inc(std_set, 1)

        deviation(0, slice(0, QT))

        def job(j):
            n, kind = index[j], j[0]
            if kind not in ACT_KINDS:
                return
            act.wait_ge(pe_done, n + 1)
            src = wide[n % 2]
            if kind == "kv":
                b, kt = j[1:]
                if kt == 0:
                    if b < 2:
                        act.wait_ge(values_prepared, 3)
                    else:
                        act.wait_ge(pv_done, 32 * (b - 1))
                nc.scalar.activation(vaug[b % 2][:, kt, :, 0:DK],
                                     src[:, 1, 0:D].rearrange("p (h d) -> p h d", h=H), ACT.Copy).then_inc(act_done, 1)
                return
            if kind in ("xT", "oT"):
                m = last_before(n, ("q", "oP"))
                if m >= 0:
                    act.wait_ge(pe_done, m + 1)
                dst, src = xT_hi[:, :, :], src[:, :, :]
            elif kind in ("trq", "trk"):
                if piece_job(j) >= 2:
                    act.wait_ge(pieces_out[piece_job(j) % 2], 16 * (piece_job(j) // 2))
                dst, src = pieces[:, piece_job(j) % 2, 0, :, :], src[:, :, :]
            else:
                if j[1] > 0:
                    act.wait_ge(maxrow_out, 16 * j[1])
                dst, src = mxp[:, 0, :], src[0:4, 0, :]
            nc.scalar.activation(dst, src, ACT.Copy).then_inc(act_done, 1)

        def exponential(g, hq):
            n = 4 * g + hq
            act.wait_ge(score_ready, n + 1)
            if n >= NP:
                act.wait_ge(pv_done, (n - NP) // 4 + 1)
            nc.scalar.activation(probs[:, n % NP, :], narrow[n % 3][:, :], ACT.Exp, scale=DK ** -0.5).then_inc(exp_done, 1)

        def take_out(quad):
            act.wait_ge(pv_done, 8 * (quad + 1))
            if quad >= 1:
                act.wait_ge(pe_done, index[("out", quad - 1)] + 1)
            nc.scalar.activation(outT[:, :], values[:, :], ACT.Copy).then_inc(outT_set, 1)

        for j in before:
            job(j)
            if j == ("kv", 0, 4):
                deviation(1, slice(QT, NT))
        for g in range(GROUPS):
            for what, n in GROUP_STEPS:
                if what == "score":
                    exponential(g, n)
                elif what == "weigh" and g % 8 == 0 and g > 0:
                    take_out(g // 8 - 1)
                elif what == "jobs":
                    for j in places[g][n]:
                        job(j)
        take_out(QUADS - 1)
        for j in after:
            job(j)

    @block.vector
    def _(dve):
        steps = [0]

        def step(ins):
            steps[0] += 1
            ins.then_inc(dve_step, 1)

        def settle():
            dve.wait_ge(dve_step, steps[0])

        nc.vector.memset(values[:, :], 0.0).then_inc(values_prepared, 1)
        def statistics(batches):
            for b in batches:
                dve.wait_ge(x_in[b], 16)
                for t in range(QT * b, QT * b + QT):
                    step(nc.vector.bn_stats(stats[:, t, :], xt[:, t, :]))
            settle()
            tiles = slice(QT * batches[0], QT * batches[-1] + QT)
            for t in range(tiles.start, tiles.stop):
                step(nc.vector.bn_aggr(mv[:, t, :], stats[:, t, :]))
            settle()
            nc.vector.tensor_scalar_add(varc[:, tiles], mv[:, tiles, 1], EPS).then_inc(var_set, 1)

        def deviations(i, tiles):
            dve.wait_ge(std_set, i + 1)
            step(nc.vector.reciprocal(rstd[:, tiles], std[:, tiles]))
            settle()

        def split_weight(w):
            dve.wait_ge(w_in[w], 16)
            step(nc.vector.tensor_copy(w_hi[w][:, :, :], wraw[w]))
            settle()
            nc.vector.tensor_tensor(w_lo[w][:, :, :], wraw[w], w_hi[w][:, :, :].bitcast(F32), ALU.subtract).then_inc(w_split, 1)

        def key_tables(b):
            for out, table in ((kcos, cos), (ksin, sin)):
                step(nc.vector.tensor_tensor(out[:, b % 2, :, :], table[:, :, :],
                                             mcol[:, KT * b:KT * b + KT].unsqueeze(2).to_broadcast([P, KT, CD]), ALU.mult))

        def normalise(b):
            for t in range(QT):
                nc.vector.tensor_scalar(xn[:, t, :], xt[:, QT * b + t, :], mv[:, QT * b + t, 0:1],
                                        rstd[:, QT * b + t:QT * b + t + 1], ALU.subtract, ALU.mult).then_inc(xn_set, 1)

        def high_part(i):
            b, g = divmod(i, 2)
            dve.wait_ge(c_in, 16 * (i + 1))
            if b > 0:
                dve.wait_ge(pe_done, index[("kv", b - 1, 4 * g + 3)] + 1)
            nc.vector.tensor_copy(c_hi[:, :, 512 * g:512 * g + 512], craw[:, :, :]).then_inc(c_high, 1)

        def masks():
            dve.wait_ge(tab_in, 96)
            step(nc.vector.tensor_scalar(mcol[:, :], mcol_i[:, :], 0.0, None, ALU.not_equal))
            nc.vector.tensor_scalar(mrow[:, :], mrow_i, 0.0, mcoef[:, 0:1], ALU.is_equal, ALU.mult).then_inc(mask_set, 1)
            settle()
            key_tables(0)

        statistics([0])
        deviations(0, slice(0, QT))
        normalise(0)
        split_weight("q")
        high_part(0)

        def job(j):
            n, kind = index[j], j[0]
            slot = wide[n % 2]
            dve.wait_ge(pe_done, n + 1)
            if kind in SPLIT:
                dve.wait_ge(act_done, act_count(n))
            if kind in PIECED or kind == "mxt":
                m = last_before(n, PIECED)
                if m >= 0:
                    dve.wait_ge(pool_done, pool_count(m))
                m = last_before(n, ("mxt",))
                if m >= 0:
                    dve.wait_ge(dve_done, m + 1)
            if kind in ("xT", "oT"):
                nc.vector.tensor_tensor(xT_lo[:, :, :], slot[:, :, :], xT_hi[:, :, :].bitcast(F32), ALU.subtract).then_inc(dve_done, 1)
                if kind == "xT" and 0 < j[1] < B - 1:
                    key_tables(j[1] + 1)
                if kind == "oT" and j[1] + 2 < B:
                    normalise(j[1] + 2)
            elif kind in ("q", "kv"):
                r = tile_number(j)
                if r >= 2:
                    before_last = [m for m in range(n) if jobs[m][0] in ("q", "kv")][-2]
                    dve.wait_ge(pool_done, pool_count(before_last))
                    if r >= 8:
                        dve.wait_ge(pe_done, transposed_by(r - 8) + 1)
                if kind == "q":
                    c, s = cos[:, j[2], :], sin[:, j[2], :]
                else:
                    c, s = kcos[:, j[1] % 2, j[2], :], ksin[:, j[1] % 2, j[2], :]
                    if j[2] == 0:
                        settle()
                a = roped[:, r % 8, :].rearrange("p (d h) -> p d h", h=HH)
                rot = rope_b[:, r % 2, :].rearrange("p (i two h) -> p i two h", two=2, h=HH)
                swapped = slot[:, 0, 0:D].rearrange("p (i two h) -> p i two h", two=2, h=HH)[:, :, ::-1, :]
                nc.vector.tensor_tensor(a, slot[:, 0, 0:D].rearrange("p (d h) -> p d h", h=HH),
                                        c.unsqueeze(2).to_broadcast([P, CD, HH]), ALU.mult)
                nc.vector.tensor_tensor(rot, swapped, s.rearrange("p (i two) -> p i two", two=2)
                                        .unsqueeze(3).to_broadcast([P, CD // 2, 2, HH]), ALU.mult).then_inc(dve_done, 1)
            elif kind in ("trq", "trk"):
                part = pieces[:, piece_job(j) % 2, :, :, :]
                step(nc.vector.tensor_tensor(rest[:, :, :], slot[:, :, :], part[:, 0, :, :], ALU.subtract))
                settle()
                nc.vector.tensor_copy(part[:, 1, :, :], rest[:, :, :]).then_inc(dve_done, 1)
            elif kind == "mxt":
                left = rest[0:4, 0, :]
                step(nc.vector.tensor_tensor(left, slot[0:4, 0, :], mxp[:, 0, :], ALU.subtract))
                settle()
                step(nc.vector.tensor_copy(mxp[:, 1, :], left))
                settle()
                nc.vector.tensor_tensor(mxp[:, 2, :], left, mxp[:, 1, :], ALU.subtract).then_inc(dve_done, 1)
            elif kind == "max":
                quad, h, qt = j[1:]
                if quad >= 2 and h == 0 and qt == 0:
                    dve.wait_ge(pe_done, index[("mxt", quad - 2)] + 1)
                nc.vector.tensor_reduce(mx[quad % 2][:, 4 * qt + h:4 * qt + h + 1], slot[:, :, :], axis=AX.XY, op=ALU.max,
                                        negate=True).then_inc(dve_done, 1)
            elif kind == "out":
                b, first = j[1] // 4, 64 * (j[1] % 4)
                if b > 0 and first == 0:
                    dve.wait_ge(pe_done, index[("oT", b - 1)] + 1)
                if j[1] > 0:
                    dve.wait_ge(dve_done, index[("out", j[1] - 1)] + 1)
                o = slot[:, 0, :].rearrange("p (q h e) -> p q h e", q=QT, e=32)
                step(nc.vector.reciprocal(rec[:, :].rearrange("p (q h e) -> p q h e", q=QT, e=1), o[:, :, :, DK:DK + 1]))
                settle()
                nc.vector.tensor_tensor(attn[:, :, first:first + 64].rearrange("p q (h d) -> p q h d", d=DK), o[:, :, :, 0:DK],
                                        rec[:, :].rearrange("p (q h e) -> p q h e", q=QT, e=1).to_broadcast([P, QT, 4, DK]),
                                        ALU.mult).then_inc(dve_done, 1)
            elif kind == "oP":
                b = j[1]
                xb = xt[:, QT * b:QT * b + QT, :]
                nc.vector.tensor_tensor(xb, slot[:, :, :].rearrange("p k (t d) -> p (k t) d", d=D), xb, ALU.add).then_inc(dve_done, 1)

        for j in jobs:
            job(j)
            if j == ("xT", 0):
                split_weight("k")
            elif j == ("q", 0, 1):
                split_weight("v")
            elif j == ("q", 0, 3):
                masks()
            elif j == ("kv", 0, 2):
                statistics(list(range(1, B)))
            elif j == ("kv", 0, 5):
                deviations(1, slice(QT, NT))
                normalise(1)
                key_tables(1)
            elif j == ("kv", 1, 1):
                split_weight("o")
            if j in high_context:
                high_part(high_context[j])

    @block.tensor
    def _(pe):
        pe.wait_ge(tab_in, 96)

        def project(out, hi, lo, t, w, cols=slice(0, D)):
            for i, (a, c) in enumerate(((hi, w_hi[w]), (hi, w_lo[w]), (lo, w_hi[w]))):
                for k in range(KC):
                    last = nc.tensor.matmul(out, a[:, k, P * t:P * t + P], c[:, k, cols],
                                            start=(i, k) == (0, 0), stop=(i, k) == (2, KC - 1))
            return last

        def job(j):
            n, kind = index[j], j[0]
            slot = wide[n % 2]
            if n >= 2:
                pe.wait_ge(dve_done, n - 1)
                if jobs[n - 2][0] == "kv":
                    pe.wait_ge(act_done, act_count(n - 2))
            if kind == "xT":
                pe.wait_ge(xn_set, QT * (j[1] + 1))
                for k in range(KC):
                    for t in range(QT):
                        last = nc.tensor.transpose(slot[:, k, P * t:P * t + P], xn[:, t, P * k:P * k + P], ident[:, :])
            elif kind == "q":
                if j[2] == 0:
                    m = index[("xT", j[1])]
                    pe.wait_ge(dve_done, m + 1)
                    pe.wait_ge(w_split, 1)
                last = project(slot[:, 0, 0:D], xT_hi, xT_lo, j[2], "q")
            elif kind == "kv":
                if j[2] == 0:
                    pe.wait_ge(c_split, j[1] + 1)
                    pe.wait_ge(w_split, 3)
                project(slot[:, 0, 0:D], c_hi, c_lo, j[2], "k")
                last = project(slot[:, 1, 0:D], c_hi, c_lo, j[2], "v")
            elif kind in ("trq", "trk"):
                b = j[1]
                first = (QT + KT) * b + (0 if kind == "trq" else QT + 4 * j[2])
                pe.wait_ge(pool_done, pool_count(last_before(n, ("q", "kv"))))
                for k in range(KC):
                    for t in range(4):
                        last = nc.tensor.transpose(slot[:, k, P * t:P * t + P], roped[:, (first + t) % 8, P * k:P * k + P], ident[:, :])
            elif kind == "max":
                quad, h, qt = j[1:]
                u, h = quad // 2, 4 * (quad % 2) + h
                if h == 0 and qt == 0:
                    pe.wait_ge(stack_in[u % 3], STACK * (u // 3 + 1))
                for k in range(2):
                    last = nc.tensor.matmul(slot[:, k, :], qst[u % 3][0:R_MAX, h, P * qt:P * qt + P],
                                            kst[u % 3][0:R_MAX, h, 512 * k:512 * k + 512], start=True, stop=True)
            elif kind == "mxt":
                pe.wait_ge(dve_done, n)
                for qt in range(QT):
                    last = nc.tensor.transpose(slot[0:4, 0, P * qt:P * qt + P], mx[j[1] % 2][:, 4 * qt:4 * qt + 4], ident[:, :])
            elif kind == "out":
                pe.wait_ge(outT_set, j[1] + 1)
                for qt in range(QT):
                    last = nc.tensor.transpose(slot[:, 0, P * qt:P * qt + P], outT[:, P * qt:P * qt + P], ident[:, :])
            elif kind == "oT":
                pe.wait_ge(dve_done, index[("out", 4 * j[1] + 3)] + 1)
                for k in range(KC):
                    for t in range(QT):
                        last = nc.tensor.transpose(slot[:, k, P * t:P * t + P], attn[:, t, P * k:P * k + P], ident[:, :])
            elif kind == "oP":
                pe.wait_ge(dve_done, index[("oT", j[1])] + 1)
                pe.wait_ge(w_split, 4)
                for t in range(QT):
                    last = project(slot[:, t // 2, D * (t % 2):D * (t % 2) + D], aT_hi, aT_lo, t, "o")
            last.then_inc(pe_done, 1)

        def score(g, hq):
            u, quad, kt = g // 16, g // 8, g % 8
            n, h = 4 * g + hq, 4 * (quad % 2) + hq
            if kt == 0 and hq == 0:
                pe.wait_ge(maxrow_in[quad % 2], 16 * (quad // 2 + 1))
            if n >= 3:
                pe.wait_ge(exp_done, n - 2)
            nc.tensor.matmul(narrow[n % 3][:, :], kst[u % 3][0:R_ALL, h, P * kt:P * kt + P],
                             qst[u % 3][0:R_ALL, h, :], start=True, stop=True).then_inc(score_ready, 1)

        def weigh(g):
            b, kt = g // 32, g % 8
            pe.wait_ge(exp_done, 4 * g + 4)
            if g == 0:
                pe.wait_ge(values_prepared, 3)
            if g % 32 == 0:
                pe.wait_ge(act_done, act_count(index[("kv", b, KT - 1)]))
            if kt == 0 and g > 0:
                pe.wait_ge(outT_set, g // 8)
            for hq in range(4):
                h = 4 * (g // 8 % 4) + hq
                last = nc.tensor.matmul(values[32 * hq:32 * hq + DK + 1, :], vaug[b % 2][:, kt, h, :], probs[:, (4 * g + hq) % NP, :],
                                        start=kt == 0, stop=kt == KT - 1)
            last.then_inc(pv_done, 1)

        for j in before:
            job(j)
        for g in range(GROUPS):
            for what, n in GROUP_STEPS:
                if what == "score":
                    score(g, n)
                elif what == "weigh" and g >= 1:
                    weigh(g - 1)
                elif what == "jobs":
                    for j in places[g][n]:
                        job(j)
        weigh(GROUPS - 1)
        for j in after:
            job(j)


E_, F, EH = 8, 512, 4
FC = F // P
REP = H // EH
QKV = D + 2 * EH * DK
LEAST = -3.4028234663852886e38
RING = 4


PRODUCT_TIME = {"up": 1.3, "down": 2.6}


def latency(item):
    return {"stats": 2, "root": 1, "first": 1.3, "keep": 1.3, "moments": 3., "again": 1., "rates": 1., "norm": 1.27, "turn": 1, "qkv": 0.5, "score": 0.9 * (item[-1] + 1), "exps": 5, "shares": 3,
            "mix": 0.96 * (item[-1] + 1), "out": 0.8, "router": 2.8, "gates": 2}[item[0]]


def second_block_order():
    def merge(a, b):
        out, ta, tb, a, b = [], 0.0, 0.0, list(a), list(b)
        while a or b:
            if b and (not a or tb <= ta):
                tb += latency(b[0])
                out.append(b.pop(0))
            else:
                ta += latency(a[0])
                out.append(a.pop(0))
        return out

    def begin(j):
        return [("first", j)]

    def keep(j):
        return [("keep", j)]

    def moments(g):
        return [("moments", g), ("root", g, 0), ("again", g), ("root", g, 1), ("rates", g)]

    def turns(j, r):
        return [("turn", j, r, 0), ("turn", j, r, 1)]

    def scores(j):
        return [x for s in range(B) for x in (("qkv", j, s), ("score", j, s))]

    def attend(j):
        return [("exps", j), ("shares", j)] + [("mix", j, s) for s in range(B)]

    def project(j):
        return turns(j, 1) + [("out", j, s) for s in range(B)]

    def end(j):
        return [("stats", j, 2), ("root", j, 2), ("norm", j, 2)] + turns(j, 2) + [("router", j), ("gates", j)]

    beside = [scores(1) + attend(1)[:3] + keep(1) + attend(1)[3:] + merge(project(1), begin(2)) + merge(turns(2, 0) + scores(2), end(1)),
              attend(2)[:3] + keep(2) + attend(2)[3:] + merge(project(2), begin(3)) + merge(turns(3, 0) + scores(3), end(2)),
              attend(3)[:3] + keep(3) + attend(3)[3:] + project(3) + end(3), []]

    def up(u):
        return [("up", *u, f) for f in range(FC)]

    def down(u):
        items = [("down", *u, pair) for pair in range(2)]
        if u[1] == QT - 1 and u[0] + RING < E_:
            items += [("expert", u[0] + RING, 0), ("expert", u[0] + RING, 1)]
        return items

    order = []
    for item in moments(0) + begin(0) + turns(0, 0) + merge(scores(0), moments(1)) + attend(0)[:3] + begin(1) + attend(0)[3:4] + keep(0) + attend(0)[4:] + project(0) + turns(1, 0) + end(0):
        order.append(item)
        if item == ("first", 0):
            order += [("weights", 0), ("weights", 1)]
        for e, behind in enumerate((("score", 0, B - 1), ("mix", 0, B - 1), ("out", 0, B - 1))):
            if item == behind:
                order += [("expert", e, 0), ("expert", e, 1)]
    units = [(e, c) for c in range(QT) for e in range(RING)] + [(e, c) for e in range(RING, E_) for c in range(QT)]
    order += up(units[0])
    for c in range(QT):
        between = []
        for n in range(RING * c, RING * c + RING - 1):
            between += up(units[n + 1])
            if n + 3 < RING:
                between += [("expert", n + 3, 0), ("expert", n + 3, 1)]
            between += down(units[n])
        n = RING * c + RING - 1
        if c < QT - 1:
            between += down(units[n])
        else:
            between += up(units[n + 1]) + down(units[n])
        todo = beside[c]
        at, whole = 0.0, sum(latency(i) for i in todo)
        spent, length = 0.0, sum(PRODUCT_TIME.get(i[0], 0) for i in between)
        for item in between:
            order.append(item)
            spent += PRODUCT_TIME.get(item[0], 0)
            while todo and at / whole < spent / length:
                at += latency(todo[0])
                order.append(todo.pop(0))
        order += todo
        if c < QT - 1:
            order += up(units[n + 1])
    for n in range(RING * QT, len(units)):
        if n + 1 < len(units):
            order += up(units[n + 1])
        order += down(units[n])
    return order, units


def second_block(nc, ctx, io, xt, wide, narrow, values, out):
    order, units = second_block_order()
    index = {item: n for n, item in enumerate(order)}

    def sb(name, shape, dt=F32):
        return ctx.enter_context(nc.sbuf_tensor(name, shape, dt))

    def sem(name):
        return ctx.enter_context(nc.semaphore(name))

    ident = sb("ident2", [P, P])
    raw = [sb("raw1", [P, KC, F]), sb("raw2", [P, FC, D])]
    router = sb("router", [P, KC, E_])
    w1_hi = [sb(f"w1_hi{i}", [P, KC, F], F32R) for i in range(RING)]
    w1_lo = [sb(f"w1_lo{i}", [P, KC, F], F32R) for i in range(RING)]
    w2_hi = [sb(f"w2_hi{i}", [P, FC, D], F32R) for i in range(RING)]
    w2_lo = [sb(f"w2_lo{i}", [P, FC, D], F32R) for i in range(RING)]
    qkvw_hi, qkvw_lo = sb("qkvw_hi", [P, KC, QKV], F32R), sb("qkvw_lo", [P, KC, QKV], F32R)
    projw_hi, projw_lo = sb("projw_hi", [P, KC, D], F32R), sb("projw_lo", [P, KC, D], F32R)
    lncol = sb("lncol", [P, 4, KC])
    iota = sb("iota", [P, E_])
    mv1 = sb("mv1", [P, QT, B, 2])
    var1, std1 = sb("var1", [P, QT, B]), sb("std1", [P, QT, B])
    rate1, rate2 = sb("rate1", [P, QT, B]), sb("rate2", [P, QT, B])
    mv = sb("mv2", [P, B, 2])
    varc, std, rstd = sb("varc2", [P, B]), sb("std2", [P, B]), sb("rstd2", [P, B])
    hs = [sb(f"h{i}", [P, B, D]) for i in range(2)]
    norm = sb("norm", [P, B, D])
    full = sb("full", [P, KC, 512])
    yT_hi, yT_lo = sb("yT_hi", [P, KC, 512], F32R), sb("yT_lo", [P, KC, 512], F32R)
    qkv = sb("qkv", [P, B, QKV])
    prod = [sb(f"prod{i}", [P, B, D]) for i in range(2)]
    sc = sb("sc", [P, B, B, H])
    share = sc
    top, den = sb("top", [P, B, H]), sb("den", [P, B, H])
    ao = sb("ao", [P, B, D])
    stats1 = ao[:, 0, 0:QT * B * 6].rearrange("p (t s n) -> p t s n", t=QT, n=6)
    logits = sb("logits", [P, B, E_])
    stats = logits[:, :, 0:6]
    lmax, gsum = sb("lmax", [P, B]), sb("gsum", [P, B])
    best = sb("best", [P, B, 8])
    which = sb("which", [P, B, 8], mybir.dt.uint32)
    chosen = sb("chosen", [P, 2, B, E_])
    gates = sb("gates", [P, NT, E_])
    y2_hi, y2_lo = sb("y2_hi", [P, KC, NT * P], F32R), sb("y2_lo", [P, KC, NT * P], F32R)
    hid_hi = [sb(f"hid_hi{i}", [P, FC, 512], F32R) for i in range(2)]
    hid_lo = [sb(f"hid_lo{i}", [P, FC, 512], F32R) for i in range(2)]
    up_banks = [wide[f // 2][:, f % 2, :] for f in range(FC)]
    down_banks = [narrow[0], narrow[1]]
    path_banks = [narrow[2], values]
    xv = xt[:, :, :].rearrange("p (s t) d -> p s t d", s=B)
    gv = gates[:, :, :].rearrange("p (s t) e -> p s t e", s=B)
    weights = ((raw[0][:, :, 0:QKV], qkvw_hi, qkvw_lo), (raw[1][:, 0:KC, :], projw_hi, projw_lo))

    pe_done, act_done, dve_done, pool_done = sem("pe_done2"), sem("act_done2"), sem("dve_done2"), sem("pool_done2")
    act_step, dve_step, pool_step = sem("act_step2"), sem("dve_step2"), sem("pool_step2")
    const_in, router_in, raw_in = sem("const_in2"), sem("router_in"), [sem("raw1_in"), sem("raw2_in")]
    stored = sem("stored")

    ON_PE = ("turn", "qkv", "out", "router", "up", "down")
    ON_ACT = ("weights", "expert", "root", "turn", "qkv", "exps", "router", "up")
    ON_DVE = ("weights", "moments", "again", "rates", "stats", "first", "keep", "norm", "turn", "score", "exps", "shares", "mix", "out", "router", "gates", "up", "down")
    ON_POOL = ("expert", "score", "mix", "out")

    def alone(item):
        return item[0] in ("score", "mix") and item[2] == B - 1

    def count(kinds, item):
        assert item[0] in kinds and item in index, item
        return sum(i[0] in kinds and not (kinds is ON_POOL and alone(i)) for i in order[:index[item] + 1])

    def by_pe(item):
        return pe_done, count(ON_PE, item)

    def by_act(item):
        return act_done, count(ON_ACT, item)

    def by_dve(item):
        return dve_done, count(ON_DVE, item)

    def by_pool(item):
        return pool_done, count(ON_POOL, item)

    def bank(item):
        return 0 if item[0] == "router" else item[-1] % 2

    on_path = [i for i in order if i[0] in ("turn", "qkv", "out", "router")]

    def last_read(item):
        before = [i for i in on_path[:on_path.index(item)] if bank(i) == bank(item)]
        if not before:
            return None
        return by_act(before[-1]) if before[-1][0] == "qkv" or (before[-1][0] == "turn" and before[-1][2] != 1) else by_dve(before[-1])

    def full_read(item):
        n = index[item]
        before = [i for i in order[:n] if i[0] == "turn" and i[2] != 1 and i[3] == item[3]]
        if not before:
            return None
        return by_dve(before[-1]) if before[-1][2] == 0 else by_pe(("router", before[-1][1]))

    def norm_read(item):
        before = [i for i in order[:index[item]] if i[0] in ("first", "norm")]
        return by_pe(("turn", before[-1][1], 0 if before[-1][0] == "first" else 2, 1)) if before else None

    products = [i for i in order if i[0] in ("score", "mix")]

    block = ctx.enter_context(nc.Block())

    @block.sync
    def _(sp):
        sp.dma_start(ident[:, :], io["ident"]).then_inc(const_in, 16)
        sp.dma_start(lncol[:, :, :], io["lncol"]).then_inc(const_in, 16)
        sp.dma_start(iota[:, :], io["iota"]).then_inc(const_in, 16)
        sp.dma_start(weights[0][0], io["wqkv"].rearrange("(k p) n -> p k n", p=P)).then_inc(raw_in[0], 16)
        sp.dma_start(weights[1][0], io["wproj"].rearrange("(k p) n -> p k n", p=P)).then_inc(raw_in[1], 16)
        sp.dma_start(router[:, :, :], io["router"].rearrange("(k p) n -> p k n", p=P)).then_inc(router_in, 16)
        for e in range(E_):
            for i, name in enumerate(("w1", "w2")):
                sp.wait_ge(*(by_dve(("weights", i)) if e == 0 else by_pool(("expert", e - 1, i))))
                sp.dma_start(raw[i][:, :, :], io[name][e].rearrange("(k p) n -> p k n", p=P)).then_inc(raw_in[i], 16)
        rows = out.rearrange("(s t p) d -> t p s d", s=B, p=P)
        for c in range(QT):
            sp.wait_ge(*by_dve(("down", E_ - 1, c, 1)))
            sp.dma_start(rows[c], xv[:, :, c, :]).then_inc(stored, 16)
        sp.wait_ge(stored, 16 * QT)

    def shared(j, s, a):
        return qkv[:, s, a:a + EH * DK].rearrange("p (g r d) -> p g r d", g=EH, r=1).to_broadcast([P, EH, REP, DK])

    def by_group(a):
        return a.rearrange("p (g r d) -> p g r d", g=EH, r=REP)

    def group(g):
        return slice(0, 1) if g == 0 else slice(1, QT)

    def multiply(engine, item, buf):
        kind, j, s = item
        for t in range(s + 1):
            if kind == "score":
                last = engine.tensor_tensor(by_group(buf[:, t, :]), by_group(qkv[:, s, 0:D]), shared(j, t, D), ALU.mult)
            else:
                weight = share[:, s, t, :].rearrange("p (g r d) -> p g r d", g=EH, d=1).to_broadcast([P, EH, REP, DK])
                last = engine.tensor_tensor(by_group(buf[:, t, :]), weight, shared(j, t, D + EH * DK), ALU.mult)
        return last

    @block.gpsimd
    def _(pool):
        def expert(e, i):
            hi, lo = (w1_hi, w1_lo) if i == 0 else (w2_hi, w2_lo)
            pool.wait_ge(*by_act(("expert", e, i)))
            nc.gpsimd.tensor_tensor(lo[e % RING][:, :, :], raw[i][:, :, :], hi[e % RING][:, :, :].bitcast(F32), ALU.subtract).then_inc(pool_done, 1)

        def buffer(item):
            n = products.index(item)
            if n >= 2:
                pool.wait_ge(*by_dve(products[n - 2]))
            return prod[n % 2]

        for item in order:
            kind = item[0]
            if kind == "expert":
                expert(*item[1:])
            elif kind in ("score", "mix") and not alone(item):
                j, s = item[1:]
                buf = buffer(item)
                pool.wait_ge(*(by_act(("qkv", j, s)) if kind == "score" else by_dve(("shares", j))))
                last = multiply(nc.gpsimd, item, buf)
                if kind == "mix" and s < B - 1:
                    last = nc.gpsimd.memset(sc[:, s, s + 1:B, :], LEAST)
                last.then_inc(pool_done, 1)
            elif kind == "out":
                j, s = item[1:]
                pool.wait_ge(*by_dve(item))
                nc.gpsimd.tensor_tensor(xv[:, s, j, :], xv[:, s, j, :], hs[j % 2][:, s, :], ALU.add).then_inc(pool_done, 1)

    @block.scalar
    def _(act):
        steps = 0
        for item in order:
            kind = item[0]
            if kind == "weights":
                n = item[1]
                src, hi, _ = weights[n]
                act.wait_ge(raw_in[n], 16)
                nc.scalar.activation(hi[:, :, :], src, ACT.Copy).then_inc(act_done, 1)
            elif kind == "expert":
                e, i = item[1:]
                act.wait_ge(raw_in[i], 16 * (e + 2))
                if e >= RING:
                    act.wait_ge(*by_pe(("down", e - RING, QT - 1, 1)))
                nc.scalar.activation((w1_hi, w2_hi)[i][e % RING][:, :, :], raw[i][:, :, :], ACT.Copy).then_inc(act_done, 1)
            elif kind == "root":
                j, r = item[1:]
                act.wait_ge(*by_dve((("moments", j), ("again", j), ("stats", j, 2))[r]))
                if r < 2:
                    nc.scalar.activation(std1[:, group(j), :], var1[:, group(j), :], ACT.Sqrt).then_inc(act_done, 1)
                else:
                    nc.scalar.activation(std[:, :], varc[:, :], ACT.Sqrt).then_inc(act_done, 1)
            elif kind == "turn":
                j, r, k = item[1:]
                act.wait_ge(*by_pe(item))
                if (j, r, k) == (0, 0, 0):
                    act.wait_ge(const_in, 48)
                src = path_banks[bank(item)][:, :]
                if r < 2 and (j, r) != (0, 0):
                    act.wait_ge(*by_pe(("out", j - 1, B - 1) if r == 0 else ("qkv", j, B - 1)))
                if r == 1:
                    nc.scalar.activation(yT_hi[:, k, :], src, ACT.Copy).then_inc(act_done, 1)
                    continue
                if full_read(item):
                    act.wait_ge(*full_read(item))
                affine = {"scale": lncol[:, r, k:k + 1], "bias": lncol[:, r + 1, k:k + 1]}
                hi = yT_hi[:, k, :] if r == 0 else y2_hi[:, k, 512 * j:512 * j + 512]
                nc.scalar.activation(full[:, k, :], src, ACT.Identity, **affine)
                nc.scalar.activation(hi, src, ACT.Identity, **affine).then_inc(act_done, 1)
            elif kind == "qkv":
                j, s = item[1:]
                act.wait_ge(*by_pe(item))
                if j > 0:
                    act.wait_ge(*by_dve(("mix", j - 1, B - 1)))
                nc.scalar.activation(qkv[:, s, :], path_banks[bank(item)][:, 0:QKV], ACT.Copy).then_inc(act_done, 1)
            elif kind == "exps":
                act.wait_ge(*by_dve(item))
                nc.scalar.activation(share[:, :, :, :], share[:, :, :, :], ACT.Exp, scale=DK ** -0.5).then_inc(act_done, 1)
            elif kind == "router":
                act.wait_ge(*by_dve(item))
                nc.scalar.activation(logits[:, :, :], logits[:, :, :], ACT.Exp).then_inc(act_done, 1)
            elif kind == "up":
                e, c, f = item[1:]
                n = units.index((e, c))
                act.wait_ge(*by_pe(item))
                nc.scalar.activation(up_banks[f], up_banks[f], ACT.Gelu_apprx_tanh).then_inc(act_step, 1)
                steps += 1
                if n >= 2:
                    act.wait_ge(*by_pe(("down", *units[n - 2], 1)))
                act.wait_ge(act_step, steps)
                nc.scalar.activation(hid_hi[n % 2][:, f, :], up_banks[f], ACT.Copy).then_inc(act_done, 1)

    @block.vector
    def _(dve):
        steps = [0]

        def step(ins):
            steps[0] += 1
            ins.then_inc(dve_step, 1)

        def settle():
            dve.wait_ge(dve_step, steps[0])

        def variances(tile):
            for s in range(B):
                step(nc.vector.bn_stats(stats[:, s, :], tile(s)))
            settle()
            for s in range(B):
                step(nc.vector.bn_aggr(mv[:, s, :], stats[:, s, :]))
            settle()
            return nc.vector.tensor_scalar_add(varc[:, :], mv[:, :, 1], EPS)

        def normalise(dst, tile):
            step(nc.vector.reciprocal(rstd[:, :], std[:, :]))
            settle()
            for s in range(B):
                last = nc.vector.tensor_scalar(dst[:, s, :], tile(s), mv[:, s, 0:1], rstd[:, s:s + 1], ALU.subtract, ALU.mult)
            return last

        step(nc.vector.memset(sc[:, :, :, :], LEAST))
        settle()
        own = 0
        for item in order:
            kind = item[0]
            if kind not in ON_DVE:
                continue
            if kind not in ("up", "down"):
                if own > 0:
                    dve.wait_ge(dve_done, own)
            own += 1
            if kind == "weights":
                src, hi, lo = weights[item[1]]
                dve.wait_ge(*by_act(item))
                last = nc.vector.tensor_tensor(lo[:, :, :], src, hi[:, :, :].bitcast(F32), ALU.subtract)
            elif kind == "stats":
                j, r = item[1:]
                last = variances(lambda s: hs[j % 2][:, s, :])
            elif kind == "moments":
                g = group(item[1])
                tiles = [(t, s) for t in range(g.start, g.stop) for s in range(B)]
                for t, s in tiles:
                    step(nc.vector.bn_stats(stats1[:, t, s, :], xv[:, s, t, :]))
                settle()
                for t, s in tiles:
                    step(nc.vector.bn_aggr(mv1[:, t, s, :], stats1[:, t, s, :]))
                settle()
                last = nc.vector.tensor_scalar_add(var1[:, g, :], mv1[:, g, :, 1], EPS)
            elif kind == "again":
                g = group(item[1])
                dve.wait_ge(*by_act(("root", item[1], 0)))
                step(nc.vector.reciprocal(rate1[:, g, :], std1[:, g, :]))
                settle()
                step(nc.vector.tensor_tensor(var1[:, g, :], mv1[:, g, :, 1], rate1[:, g, :], ALU.mult))
                settle()
                step(nc.vector.tensor_tensor(var1[:, g, :], var1[:, g, :], rate1[:, g, :], ALU.mult))
                settle()
                last = nc.vector.tensor_scalar_add(var1[:, g, :], var1[:, g, :], EPS)
            elif kind == "rates":
                g = group(item[1])
                dve.wait_ge(*by_act(("root", item[1], 1)))
                step(nc.vector.reciprocal(rate2[:, g, :], std1[:, g, :]))
                settle()
                last = nc.vector.tensor_tensor(rate2[:, g, :], rate2[:, g, :], rate1[:, g, :], ALU.mult)
            elif kind == "first":
                j = item[1]
                if norm_read(item):
                    dve.wait_ge(*norm_read(item))
                for s in range(B):
                    last = nc.vector.tensor_scalar(norm[:, s, :], xv[:, s, j, :], mv1[:, j, s, 0:1], rate2[:, j, s:s + 1], ALU.subtract, ALU.mult)
            elif kind == "keep":
                j = item[1]
                if j > 1:
                    dve.wait_ge(*by_pool(("out", j - 2, B - 1)))
                for s in range(B):
                    last = nc.vector.tensor_scalar(hs[j % 2][:, s, :], xv[:, s, j, :], mv1[:, j, s, 0:1], rate1[:, j, s:s + 1], ALU.subtract, ALU.mult)
            elif kind == "norm":
                j, r = item[1:]
                dve.wait_ge(*by_act(("root", j, r)))
                if norm_read(item):
                    dve.wait_ge(*norm_read(item))
                last = normalise(norm, lambda s: hs[j % 2][:, s, :])
            elif kind == "turn":
                j, r, k = item[1:]
                dve.wait_ge(*by_act(item))
                if r == 1:
                    last = nc.vector.tensor_tensor(yT_lo[:, k, :], path_banks[bank(item)][:, :], yT_hi[:, k, :].bitcast(F32), ALU.subtract)
                elif r == 0:
                    last = nc.vector.tensor_tensor(yT_lo[:, k, :], full[:, k, :], yT_hi[:, k, :].bitcast(F32), ALU.subtract)
                else:
                    part = slice(512 * j, 512 * j + 512)
                    last = nc.vector.tensor_tensor(y2_lo[:, k, part], full[:, k, :], y2_hi[:, k, part].bitcast(F32), ALU.subtract)
            elif kind == "score":
                j, s = item[1:]
                buf = prod[products.index(item) % 2]
                if alone(item):
                    dve.wait_ge(*by_act(("qkv", j, s)))
                    step(multiply(nc.vector, item, buf))
                    settle()
                else:
                    dve.wait_ge(*by_pool(item))
                last = nc.vector.tensor_reduce(sc[:, s, 0:s + 1, :], buf[:, 0:s + 1, :].rearrange("p t (h d) -> p t h d", h=H),
                                               axis=AX.X, op=ALU.add)
            elif kind == "exps":
                j = item[1]
                if j > 0:
                    dve.wait_ge(*by_pool(("mix", j - 1, B - 2)))
                step(nc.vector.tensor_reduce(top[:, :, :], sc[:, :, :, :].rearrange("p s t h -> p s h t"), axis=AX.X, op=ALU.max))
                settle()
                last = nc.vector.tensor_tensor(share[:, :, :, :], sc[:, :, :, :], top[:, :, :].unsqueeze(2).to_broadcast([P, B, B, H]), ALU.subtract)
            elif kind == "shares":
                dve.wait_ge(*by_act(("exps", item[1])))
                step(nc.vector.tensor_reduce(den[:, :, :], share[:, :, :, :].rearrange("p s t h -> p s h t"), axis=AX.X, op=ALU.add))
                settle()
                step(nc.vector.reciprocal(top[:, :, :], den[:, :, :]))
                settle()
                last = nc.vector.tensor_tensor(share[:, :, :, :], share[:, :, :, :], top[:, :, :].unsqueeze(2).to_broadcast([P, B, B, H]), ALU.mult)
            elif kind == "mix":
                j, s = item[1:]
                buf = prod[products.index(item) % 2]
                if alone(item):
                    step(multiply(nc.vector, item, buf))
                    settle()
                else:
                    dve.wait_ge(*by_pool(item))
                if j > 0:
                    dve.wait_ge(*by_pe(("turn", j - 1, 1, 1)))
                if s == 0:
                    last = nc.vector.tensor_copy(ao[:, s, :], buf[:, 0, :])
                else:
                    last = nc.vector.tensor_reduce(ao[:, s, :], buf[:, 0:s + 1, :].rearrange("p t c -> p c t"), axis=AX.X, op=ALU.add)
            elif kind == "out":
                j, s = item[1:]
                dve.wait_ge(*by_pe(item))
                h = hs[j % 2][:, s, :]
                last = nc.vector.tensor_tensor(h, path_banks[bank(item)][:, 0:D], h, ALU.add)
            elif kind == "router":
                dve.wait_ge(*by_pe(item))
                lv = path_banks[0][:, 0:B * E_].rearrange("p (s e) -> p s e", e=E_)
                step(nc.vector.tensor_reduce(lmax[:, :], lv, axis=AX.X, op=ALU.max))
                settle()
                last = nc.vector.tensor_tensor(logits[:, :, :], lv, lmax[:, :].unsqueeze(2).to_broadcast([P, B, E_]), ALU.subtract)
            elif kind == "gates":
                j = item[1]

                def per_tile(a):
                    return a.unsqueeze(2).to_broadcast([P, B, E_])

                dve.wait_ge(*by_act(("router", j)))
                if j == 0:
                    dve.wait_ge(const_in, 48)
                step(nc.vector.tensor_reduce(gsum[:, :], logits[:, :, :], axis=AX.X, op=ALU.add))
                settle()
                step(nc.vector.reciprocal(lmax[:, :], gsum[:, :]))
                settle()
                step(nc.vector.tensor_tensor(logits[:, :, :], logits[:, :, :], per_tile(lmax[:, :]), ALU.mult))
                settle()
                for s in range(B):
                    step(nc.vector.max(best[:, s, :], logits[:, s, :]))
                settle()
                for s in range(B):
                    step(nc.vector.max_index(which[:, s, :], best[:, s, :], logits[:, s, :]))
                settle()
                for i in range(2):
                    step(nc.vector.tensor_tensor(chosen[:, i, :, :], iota[:, :].unsqueeze(1).to_broadcast([P, B, E_]), per_tile(which[:, :, i]), ALU.is_equal))
                settle()
                for i in range(2):
                    step(nc.vector.tensor_tensor(chosen[:, i, :, :], chosen[:, i, :, :], per_tile(best[:, :, i]), ALU.mult))
                settle()
                last = nc.vector.tensor_tensor(gv[:, :, j, :], chosen[:, 0, :, :], chosen[:, 1, :, :], ALU.add)
            elif kind == "up":
                e, c, f = item[1:]
                dve.wait_ge(*by_act(item))
                n = units.index((e, c))
                last = nc.vector.tensor_tensor(hid_lo[n % 2][:, f, :], up_banks[f], hid_hi[n % 2][:, f, :].bitcast(F32), ALU.subtract)
            else:
                e, c, pair = item[1:]
                dve.wait_ge(*by_pe(item))
                if e == 0:
                    dve.wait_ge(*by_dve(("gates", c)))
                    dve.wait_ge(*by_pool(("out", c, B - 1)))
                else:
                    dve.wait_ge(*by_dve(("down", e - 1, c, pair)))
                for i in range(2):
                    s = 2 * pair + i
                    last = nc.vector.scalar_tensor_tensor(out=xv[:, s, c, :], in0=down_banks[pair][:, D * i:D * i + D], scalar=gv[:, s, c, e:e + 1],
                                                          in1=xv[:, s, c, :], op0=ALU.mult, op1=ALU.add)
            last.then_inc(dve_done, 1)

    @block.tensor
    def _(pe):
        pe.wait_ge(const_in, 48)

        def product(dst, hi, lo, cols, w_hi, w_lo):
            chunks = hi.shape[1]
            for i, (a, w) in enumerate(((hi, w_hi), (hi, w_lo), (lo, w_hi))):
                for k in range(chunks):
                    last = nc.tensor.matmul(dst, a[:, k, cols], w[:, k, :], start=(i, k) == (0, 0), stop=(i, k) == (2, chunks - 1))
            return last

        for item in order:
            kind = item[0]
            if kind in ("turn", "qkv", "out", "router"):
                if last_read(item):
                    pe.wait_ge(*last_read(item))
                dst = path_banks[bank(item)]
            if kind == "turn":
                j, r, k = item[1:]
                pe.wait_ge(*by_dve((("first", j), ("mix", j, B - 1), ("norm", j, 2))[r]))
                src = ao if r == 1 else norm
                for s in range(B):
                    last = nc.tensor.transpose(dst[:, P * s:P * s + P], src[:, s, P * k:P * k + P], ident[:, :])
            elif kind == "qkv":
                j, s = item[1:]
                pe.wait_ge(*by_dve(("turn", j, 0, 1)))
                last = product(dst[:, 0:QKV], yT_hi, yT_lo, slice(P * s, P * s + P), qkvw_hi, qkvw_lo)
            elif kind == "out":
                j, s = item[1:]
                pe.wait_ge(*by_dve(("turn", j, 1, 1)))
                last = product(dst[:, 0:D], yT_hi, yT_lo, slice(P * s, P * s + P), projw_hi, projw_lo)
            elif kind == "router":
                j = item[1]
                pe.wait_ge(*by_dve(("turn", j, 2, 1)))
                pe.wait_ge(router_in, 16)
                for s in range(B):
                    for k in range(KC):
                        last = nc.tensor.matmul(dst[:, E_ * s:E_ * s + E_], full[:, k, P * s:P * s + P], router[:, k, :], start=k == 0, stop=k == KC - 1)
            elif kind == "up":
                e, c, f = item[1:]
                n = units.index((e, c))
                if f == 0:
                    pe.wait_ge(*by_pool(("expert", e, 0)))
                    pe.wait_ge(*by_dve(("turn", c, 2, 1)))
                if n > 0:
                    pe.wait_ge(*by_dve(("up", *units[n - 1], f)))
                rows, cols = slice(P * f, P * f + P), slice(512 * c, 512 * c + 512)
                for i, (w, y) in enumerate(((w1_hi, y2_hi), (w1_hi, y2_lo), (w1_lo, y2_hi))):
                    for k in range(KC):
                        last = nc.tensor.matmul(up_banks[f], w[e % RING][:, k, rows], y[:, k, cols], start=(i, k) == (0, 0), stop=(i, k) == (2, KC - 1))
            elif kind == "down":
                e, c, pair = item[1:]
                n = units.index((e, c))
                if pair == 0:
                    pe.wait_ge(*by_pool(("expert", e, 1)))
                    pe.wait_ge(*by_dve(("up", e, c, FC - 1)))
                if n > 0:
                    pe.wait_ge(*by_dve(("down", *units[n - 1], pair)))
                for i in range(2):
                    s = 2 * pair + i
                    last = product(down_banks[pair][:, D * i:D * i + D], hid_hi[n % 2], hid_lo[n % 2], slice(P * s, P * s + P),
                                   w2_hi[e % RING], w2_lo[e % RING])
            else:
                continue
            last.then_inc(pe_done, 1)


def tables():
    inv = 1.0 / np.float32(10000.0) ** (np.arange(0, DK, 2, dtype=np.float32) / DK)
    ang = np.repeat(np.arange(SK, dtype=np.float32)[:, None] * inv.astype(np.float32)[None, :], 2, axis=-1)
    sign = np.where(np.arange(DK) % 2 == 0, -1.0, 1.0).astype(np.float32)
    c, s = (np.tile(v, (1, CD // DK)).reshape(KT, P, CD).transpose(1, 0, 2) for v in (np.cos(ang), np.sin(ang) * sign))
    return {"cos": np.ascontiguousarray(c), "sin": np.ascontiguousarray(s), "ident": np.eye(P, dtype=np.float32),
            "iota": np.tile(np.arange(E_, dtype=np.float32), (P, 1)),
            "mask_coef": np.tile(np.array(MASK_PARTS, np.float32), B)[:, None]}


def program(nc, io, out):
    with ExitStack() as ctx:
        xt = ctx.enter_context(nc.sbuf_tensor("xt", [P, NT, D], F32))
        wide = [ctx.enter_context(nc.psum_tensor(f"wide{i}", [P, 2, 512], F32)) for i in range(2)]
        narrow = [ctx.enter_context(nc.psum_tensor(f"narrow{i}", [P, 512], F32)) for i in range(3)]
        values = ctx.enter_context(nc.psum_tensor("values", [P, 512], F32))
        with ExitStack() as part:
            cross_attention(nc, part, io, xt, wide, narrow, values)
        with ExitStack() as part:
            second_block(nc, part, io, xt, wide, narrow, values, out)


def kernel(**inputs):
    import concourse.bacc as _bacc
    from concourse.bass_utils import run_bass_kernel_spmd as _run

    a = {k: np.asarray(v) for k, v in inputs.items()}
    T = np.ascontiguousarray
    arrays = {
        "x": T(a["x"].reshape(B * SQ, D)),
        "ctxT": T(a["ctx_1024"].reshape(B * SK, D).T),
        "mask_col": T(a["mask_BxS2_ik0"].reshape(B * KT, P).T),
        "mask_row": T(np.repeat(a["mask_BxS2_ik0"], 2, axis=0)),
        **{"w" + w: T(a["L0_xattn_w_" + w].reshape(2, HH, DK, D).transpose(3, 0, 2, 1).reshape(D, D)) for w in "qk"},
        **{"w" + w: T(a["L0_xattn_w_" + w].T) for w in "vo"},
        "wqkv": T(a["L0_ffn_qkv_weight"].T),
        "wproj": T(a["L0_ffn_proj_weight"].T),
        "router": T(a["L0_ffn_router_weight"].T),
        "w1": T(a["L0_ffn_moe_w1"]),
        "w2": T(a["L0_ffn_moe_w2"]),
        "lncol": T(np.stack([a["L0_ffn_ln1_weight"], a["L0_ffn_ln1_bias"], a["L0_ffn_ln2_weight"],
                             a["L0_ffn_ln2_bias"]]).reshape(4, KC, P).transpose(2, 0, 1)),
        **tables(),
    }
    nc = _bacc.Bacc("TRN2", target_bir_lowering=False, num_devices=1)
    io = {n: nc.dram_tensor("in_" + n, v.shape, mybir.dt.from_np(v.dtype), kind="ExternalInput").ap() for n, v in arrays.items()}
    out = nc.dram_tensor("out", (B * SQ, D), F32, kind="ExternalOutput").ap()
    program(nc, io, out)
    r = _run(nc, [{"in_" + n: v for n, v in arrays.items()}], core_ids=[0])
    return r.results[0]["out"].reshape(B, SQ, D)
```
